# Optimizing a Trainium2 kernel written in Bass

```python
import numpy as np
import jax
import jax.numpy as jnp

def _softmax(x, axis=-1):
    return jax.nn.softmax(x, axis=axis)

def _gelu(x):
    return jax.nn.gelu(x, approximate=True)

def _silu(x):
    return jax.nn.silu(x)

def _sigmoid(x):
    return jax.nn.sigmoid(x)

def _layernorm(x, axis=-1, eps=1e-05):
    m = jnp.mean(x, axis=axis, keepdims=True)
    v = jnp.var(x, axis=axis, keepdims=True)
    return (x - m) / jnp.sqrt(v + eps)

def _scatter_add(tgt, idx, src, axis=0):
    return tgt.at[idx].add(src)

def _segment_sum(src, seg, n):
    return jax.ops.segment_sum(src, seg, n)
kernel_name = 'mk_adaln_d1_jaxref_r4_4f21b8'

def setup_inputs(seed: int=0):
    np.random.seed(seed)
    _w = jnp.asarray

    def _L0_attn_setup():
        import jax, jax.numpy as jnp
        import numpy as np
        DIM = 256
        DIM_HEAD = 64
        HEADS = DIM // DIM_HEAD
        B, N = (2, 512)
        LN_EPS = 1e-05
        RMS_EPS = 1e-08

        def _rmsnorm(x, gamma):
            d = x.shape[-1]
            norm = jnp.linalg.norm(x, axis=-1, keepdims=True) * d ** (-0.5)
            return x / jnp.maximum(norm, RMS_EPS) * gamma

        def _layernorm(x, gamma, beta):
            mu = jnp.mean(x, axis=-1, keepdims=True)
            var = jnp.var(x, axis=-1, keepdims=True)
            return (x - mu) * jax.lax.rsqrt(var + LN_EPS) * gamma + beta
        key = jax.random.key(seed)
        ks = jax.random.split(key, 8)
        s = DIM ** (-0.5)
        return {'x': jax.random.normal(ks[0], (B, N, DIM), dtype=jnp.float32), 'ln_gamma': jnp.ones((DIM,), jnp.float32), 'ln_beta': jnp.zeros((DIM,), jnp.float32), 'q_gamma': jnp.ones((DIM_HEAD,), jnp.float32), 'k_gamma': jnp.ones((DIM_HEAD,), jnp.float32), 'w_q': jax.random.normal(ks[1], (DIM, DIM), jnp.float32) * s, 'w_k': jax.random.normal(ks[2], (DIM, DIM), jnp.float32) * s, 'w_v': jax.random.normal(ks[3], (DIM, DIM), jnp.float32) * s, 'w_o': jax.random.normal(ks[4], (DIM, DIM), jnp.float32) * s, 'b_o': jnp.zeros((DIM,), jnp.float32)}
    _L0_attn_in = _L0_attn_setup()

    def _L0_ffn_setup():
        import jax, jax.numpy as jnp
        import numpy as np
        DIM = 256
        DEPTH = 2
        HEADS = 8
        DIM_HEAD = 64
        WINDOW = 128
        INNER = HEADS * DIM_HEAD
        HID = int(DIM * 4 * 2 / 3)
        B, N = (2, 2048)
        QK_SCALE = 8.0

        def shift_token(t):
            t1, t2 = jnp.split(t, 2, axis=-1)
            t2 = jnp.pad(t2, ((0, 0), (1, 0), (0, 0)))[:, :-1]
            return jnp.concatenate([t1, t2], axis=-1)

        def l2norm(t):
            return t / jnp.clip(jnp.linalg.norm(t, axis=-1, keepdims=True), 1e-12)

        def rotate_half(x):
            x1, x2 = jnp.split(x, 2, axis=-1)
            return jnp.concatenate([-x2, x1], axis=-1)

        def rotary_xpos(q, k):
            n = q.shape[-2]
            half_idx = jnp.arange(0, DIM_HEAD, 2, dtype=jnp.float32)
            inv_freq = 1.0 / 10000.0 ** (half_idx / DIM_HEAD)
            t = jnp.arange(n, dtype=jnp.float32)
            freqs = t[:, None] * inv_freq[None, :]
            freqs = jnp.concatenate([freqs, freqs], axis=-1)
            base = (half_idx + 0.4 * DIM_HEAD) / (1.4 * DIM_HEAD)
            power = (t - n // 2) / float(WINDOW // 2)
            scale = base[None, :] ** power[:, None]
            scale = jnp.concatenate([scale, scale], axis=-1)
            cos, sin = (jnp.cos(freqs), jnp.sin(freqs))
            q = q * cos * scale + rotate_half(q) * sin * scale
            k = k * cos / scale + rotate_half(k) * sin / scale
            return (q, k)

        def local_attention(q, k, v):
            b, h, n, d = q.shape
            w = n // WINDOW
            bq = q.reshape(b, h, w, WINDOW, d) * QK_SCALE
            bk = k.reshape(b, h, w, WINDOW, d)
            bv = v.reshape(b, h, w, WINDOW, d)

            def look_around(t):
                p = jnp.pad(t, ((0, 0), (0, 0), (1, 0), (0, 0), (0, 0)))
                return jnp.concatenate([p[:, :, :w], p[:, :, 1:]], axis=3)
            bk, bv = (look_around(bk), look_around(bv))
            bt = jnp.arange(n).reshape(w, WINDOW)
            btp = jnp.pad(bt, ((1, 0), (0, 0)), constant_values=-1)
            btk = jnp.concatenate([btp[:w], btp[1:]], axis=1)
            sim = jnp.einsum('bhwid,bhwjd->bhwij', bq, bk)
            i = bt[:, :, None]
            j = btk[:, None, :]
            mask = (i < j) | (i > j + WINDOW) | (j == -1)
            sim = jnp.where(mask, -jnp.finfo(sim.dtype).max, sim)
            attn = jax.nn.softmax(sim, axis=-1)
            out = jnp.einsum('bhwij,bhwjd->bhwid', attn, bv)
            return out.reshape(b, h, n, d)

        def _layer(x, wqkv, qs, ksc, wo, lg, lb, w1, b1, w2, b2):
            b, n, _ = x.shape
            h = shift_token(x)
            qkv = h @ wqkv
            q, k, v = jnp.split(qkv, 3, axis=-1)
            to_heads = lambda t: t.reshape(b, n, HEADS, DIM_HEAD).transpose(0, 2, 1, 3)
            q, k, v = (to_heads(q), to_heads(k), to_heads(v))
            q = l2norm(q) * qs
            k = l2norm(k) * ksc
            q, k = rotary_xpos(q, k)
            o = local_attention(q, k, v)
            o = o.transpose(0, 2, 1, 3).reshape(b, n, INNER)
            x = x + o @ wo
            h = shift_token(x)
            mu = h.mean(-1, keepdims=True)
            var = h.var(-1, keepdims=True)
            h = (h - mu) / jnp.sqrt(var + 1e-05) * lg + lb
            h = h @ w1 + b1
            a, g = jnp.split(h, 2, axis=-1)
            h = a * jax.nn.gelu(g, approximate=False)
            x = x + h @ w2 + b2
            return x
        key = jax.random.key(seed)
        ks = jax.random.split(key, 6)
        return {'x': jax.random.normal(ks[0], (B, N, DIM), jnp.float32), 'wqkv': jax.random.normal(ks[1], (DEPTH, DIM, 3 * INNER), jnp.float32) * 0.02, 'q_scale': jnp.ones((DEPTH, DIM_HEAD), jnp.float32), 'k_scale': jnp.ones((DEPTH, DIM_HEAD), jnp.float32), 'wo': jax.random.normal(ks[2], (DEPTH, INNER, DIM), jnp.float32) * 0.02, 'ln_g': jnp.ones((DEPTH, DIM), jnp.float32), 'ln_b': jnp.zeros((DEPTH, DIM), jnp.float32), 'w1': jax.random.normal(ks[3], (DEPTH, DIM, 2 * HID), jnp.float32) * 0.02, 'b1': jnp.zeros((DEPTH, 2 * HID), jnp.float32), 'w2': jax.random.normal(ks[4], (DEPTH, HID, DIM), jnp.float32) * 0.02, 'b2': jnp.zeros((DEPTH, DIM), jnp.float32)}
    _L0_ffn_in = _L0_ffn_setup()
    _L0_c = _w((lambda *s: np.random.randn(*s).astype(np.float32) * 0.05)(4, 256))
    _L0_wmod = _w((lambda *s: np.random.randn(*s).astype(np.float32) * 0.05)(256, 6 * 256) * 256 ** (-0.5))
    _d = {'L0_attn_x': _L0_attn_in['x'], 'L0_attn_ln_gamma': _L0_attn_in['ln_gamma'], 'L0_attn_ln_beta': _L0_attn_in['ln_beta'], 'L0_attn_q_gamma': _L0_attn_in['q_gamma'], 'L0_attn_k_gamma': _L0_attn_in['k_gamma'], 'L0_attn_w_q': _L0_attn_in['w_q'], 'L0_attn_w_k': _L0_attn_in['w_k'], 'L0_attn_w_v': _L0_attn_in['w_v'], 'L0_attn_w_o': _L0_attn_in['w_o'], 'L0_attn_b_o': _L0_attn_in['b_o'], 'L0_ffn_wqkv': _L0_ffn_in['wqkv'], 'L0_ffn_q_scale': _L0_ffn_in['q_scale'], 'L0_ffn_k_scale': _L0_ffn_in['k_scale'], 'L0_ffn_wo': _L0_ffn_in['wo'], 'L0_ffn_ln_g': _L0_ffn_in['ln_g'], 'L0_ffn_ln_b': _L0_ffn_in['ln_b'], 'L0_ffn_w1': _L0_ffn_in['w1'], 'L0_ffn_b1': _L0_ffn_in['b1'], 'L0_ffn_w2': _L0_ffn_in['w2'], 'L0_ffn_b2': _L0_ffn_in['b2'], 'L0_c': _L0_c, 'L0_wmod': _L0_wmod}
    _x0 = _d['L0_attn_x']
    _d['L0_attn_x'] = jax.random.normal(jax.random.fold_in(jax.random.key(seed), 1), (4, 1024, 256), dtype=_x0.dtype)
    del _x0
    return _d

def reference(L0_attn_x, L0_attn_ln_gamma, L0_attn_ln_beta, L0_attn_q_gamma, L0_attn_k_gamma, L0_attn_w_q, L0_attn_w_k, L0_attn_w_v, L0_attn_w_o, L0_attn_b_o, L0_ffn_wqkv, L0_ffn_q_scale, L0_ffn_k_scale, L0_ffn_wo, L0_ffn_ln_g, L0_ffn_ln_b, L0_ffn_w1, L0_ffn_b1, L0_ffn_w2, L0_ffn_b2, L0_c, L0_wmod):

    def _L0_attn_ref(x, ln_gamma, ln_beta, q_gamma, k_gamma, w_q, w_k, w_v, w_o, b_o):
        import jax, jax.numpy as jnp
        import numpy as np
        DIM = 256
        DIM_HEAD = 64
        HEADS = DIM // DIM_HEAD
        B, N = (2, 512)
        LN_EPS = 1e-05
        RMS_EPS = 1e-08

        def _rmsnorm(x, gamma):
            d = x.shape[-1]
            norm = jnp.linalg.norm(x, axis=-1, keepdims=True) * d ** (-0.5)
            return x / jnp.maximum(norm, RMS_EPS) * gamma

        def _layernorm(x, gamma, beta):
            mu = jnp.mean(x, axis=-1, keepdims=True)
            var = jnp.var(x, axis=-1, keepdims=True)
            return (x - mu) * jax.lax.rsqrt(var + LN_EPS) * gamma + beta
        h, dh = (HEADS, DIM_HEAD)
        xn = _layernorm(x, ln_gamma, ln_beta)

        def proj(w):
            y = xn @ w.T
            b, n, _ = y.shape
            return y.reshape(b, n, h, dh).transpose(0, 2, 1, 3)
        q = proj(w_q)
        k = proj(w_k)
        v = proj(w_v)
        qn = _rmsnorm(q, q_gamma) * dh ** (-0.5)
        kn = _rmsnorm(k, k_gamma)
        sim = jnp.einsum('bhid,bhjd->bhij', qn, kn)
        attn = jax.nn.softmax(sim, axis=-1)
        out = jnp.einsum('bhij,bhjd->bhid', attn, v)
        b, _, n, _ = out.shape
        out = out.transpose(0, 2, 1, 3).reshape(b, n, h * dh)
        return out @ w_o.T + b_o

    def _L0_ffn_ref(x, wqkv, q_scale, k_scale, wo, ln_g, ln_b, w1, b1, w2, b2):
        import jax, jax.numpy as jnp
        import numpy as np
        DIM = 256
        DEPTH = 2
        HEADS = 8
        DIM_HEAD = 64
        WINDOW = 128
        INNER = HEADS * DIM_HEAD
        HID = int(DIM * 4 * 2 / 3)
        B, N = (2, 2048)
        QK_SCALE = 8.0

        def shift_token(t):
            t1, t2 = jnp.split(t, 2, axis=-1)
            t2 = jnp.pad(t2, ((0, 0), (1, 0), (0, 0)))[:, :-1]
            return jnp.concatenate([t1, t2], axis=-1)

        def l2norm(t):
            return t / jnp.clip(jnp.linalg.norm(t, axis=-1, keepdims=True), 1e-12)

        def rotate_half(x):
            x1, x2 = jnp.split(x, 2, axis=-1)
            return jnp.concatenate([-x2, x1], axis=-1)

        def rotary_xpos(q, k):
            n = q.shape[-2]
            half_idx = jnp.arange(0, DIM_HEAD, 2, dtype=jnp.float32)
            inv_freq = 1.0 / 10000.0 ** (half_idx / DIM_HEAD)
            t = jnp.arange(n, dtype=jnp.float32)
            freqs = t[:, None] * inv_freq[None, :]
            freqs = jnp.concatenate([freqs, freqs], axis=-1)
            base = (half_idx + 0.4 * DIM_HEAD) / (1.4 * DIM_HEAD)
            power = (t - n // 2) / float(WINDOW // 2)
            scale = base[None, :] ** power[:, None]
            scale = jnp.concatenate([scale, scale], axis=-1)
            cos, sin = (jnp.cos(freqs), jnp.sin(freqs))
            q = q * cos * scale + rotate_half(q) * sin * scale
            k = k * cos / scale + rotate_half(k) * sin / scale
            return (q, k)

        def local_attention(q, k, v):
            b, h, n, d = q.shape
            w = n // WINDOW
            bq = q.reshape(b, h, w, WINDOW, d) * QK_SCALE
            bk = k.reshape(b, h, w, WINDOW, d)
            bv = v.reshape(b, h, w, WINDOW, d)

            def look_around(t):
                p = jnp.pad(t, ((0, 0), (0, 0), (1, 0), (0, 0), (0, 0)))
                return jnp.concatenate([p[:, :, :w], p[:, :, 1:]], axis=3)
            bk, bv = (look_around(bk), look_around(bv))
            bt = jnp.arange(n).reshape(w, WINDOW)
            btp = jnp.pad(bt, ((1, 0), (0, 0)), constant_values=-1)
            btk = jnp.concatenate([btp[:w], btp[1:]], axis=1)
            sim = jnp.einsum('bhwid,bhwjd->bhwij', bq, bk)
            i = bt[:, :, None]
            j = btk[:, None, :]
            mask = (i < j) | (i > j + WINDOW) | (j == -1)
            sim = jnp.where(mask, -jnp.finfo(sim.dtype).max, sim)
            attn = jax.nn.softmax(sim, axis=-1)
            out = jnp.einsum('bhwij,bhwjd->bhwid', attn, bv)
            return out.reshape(b, h, n, d)

        def _layer(x, wqkv, qs, ksc, wo, lg, lb, w1, b1, w2, b2):
            b, n, _ = x.shape
            h = shift_token(x)
            qkv = h @ wqkv
            q, k, v = jnp.split(qkv, 3, axis=-1)
            to_heads = lambda t: t.reshape(b, n, HEADS, DIM_HEAD).transpose(0, 2, 1, 3)
            q, k, v = (to_heads(q), to_heads(k), to_heads(v))
            q = l2norm(q) * qs
            k = l2norm(k) * ksc
            q, k = rotary_xpos(q, k)
            o = local_attention(q, k, v)
            o = o.transpose(0, 2, 1, 3).reshape(b, n, INNER)
            x = x + o @ wo
            h = shift_token(x)
            mu = h.mean(-1, keepdims=True)
            var = h.var(-1, keepdims=True)
            h = (h - mu) / jnp.sqrt(var + 1e-05) * lg + lb
            h = h @ w1 + b1
            a, g = jnp.split(h, 2, axis=-1)
            h = a * jax.nn.gelu(g, approximate=False)
            x = x + h @ w2 + b2
            return x
        for l in range(DEPTH):
            x = _layer(x, wqkv[l], q_scale[l], k_scale[l], wo[l], ln_g[l], ln_b[l], w1[l], b1[l], w2[l], b2[l])
        return x
    x = L0_attn_x
    mod = (_silu(L0_c) @ L0_wmod).reshape(L0_c.shape[0], 6, 1, -1)
    sa, ca, ga, sb, cb, gb = (mod[:, 0], mod[:, 1], mod[:, 2], mod[:, 3], mod[:, 4], mod[:, 5])
    ga = (2 * (ga >= 0) - 1) * jnp.maximum(jnp.abs(ga), 0.25)
    gb = (2 * (gb >= 0) - 1) * jnp.maximum(jnp.abs(gb), 0.25)
    h = _layernorm(x, axis=-1) * (1 + ca) + sa
    x = x + ga * _L0_attn_ref(h, L0_attn_ln_gamma, L0_attn_ln_beta, L0_attn_q_gamma, L0_attn_k_gamma, L0_attn_w_q, L0_attn_w_k, L0_attn_w_v, L0_attn_w_o, L0_attn_b_o)
    h = _layernorm(x, axis=-1) * (1 + cb) + sb
    x = x + gb * _L0_ffn_ref(h, L0_ffn_wqkv, L0_ffn_q_scale, L0_ffn_k_scale, L0_ffn_wo, L0_ffn_ln_g, L0_ffn_ln_b, L0_ffn_w1, L0_ffn_b1, L0_ffn_w2, L0_ffn_b2)
    return x

_drawn_inputs = setup_inputs


def setup_inputs(seed=0):
    import zlib

    import numpy as np

    out = dict(_drawn_inputs(seed))
    spreads = {'L0_attn_ln_gamma': (1.0, 0.6),
     'L0_attn_ln_beta': (0.0, 0.296),
     'L0_attn_q_gamma': (1.0, 0.6),
     'L0_attn_k_gamma': (1.0, 0.6),
     'L0_attn_b_o': (0.0, 0.317),
     'L0_ffn_q_scale': (1.0, 0.6),
     'L0_ffn_k_scale': (1.0, 0.6),
     'L0_ffn_ln_g': (1.0, 0.6),
     'L0_ffn_ln_b': (0.0, 0.8),
     'L0_ffn_b1': (0.0, 0.8),
     'L0_ffn_b2': (0.0, 0.512)}
    factors = {'L0_ffn_wqkv': 6.69, 'L0_ffn_wo': 6.649, 'L0_ffn_w1': 4.706, 'L0_ffn_w2': 4.692}
    for name, (base, spread) in spreads.items():
        noise = np.random.default_rng([zlib.crc32(name.encode()), seed]).standard_normal(out[name].shape)
        drawn = base * np.exp(spread * noise) if base else spread * noise
        out[name] = jnp.asarray(drawn.astype(out[name].dtype))
    for name, factor in factors.items():
        out[name] = (out[name] * factor).astype(out[name].dtype)
    return out
```

```python
from contextlib import ExitStack

import numpy as np

import concourse.bass as bass
from concourse import mybir

F32 = mybir.dt.float32
F32R = mybir.dt.float32r
U32 = mybir.dt.uint32
I32 = mybir.dt.int32
ALU = mybir.AluOpType
ACT = mybir.ActivationFunctionType
AX = mybir.AxisListType.X

P = 128
B, N, D = 4, 1024, 256
NT = N // P
KC = D // P
GH, HD = 4, 64
HALF = N // 2
LN_EPS = 1e-5
RMS_EPS = 1e-8
MAGIC = 0x5F3759DF
RSQRT_LINKS = 11


class Slots:

    def __init__(self, order, tensors, done, release):
        self.tensors, self.done, self.release = tensors, done, release
        self.slot = {(k, i): s for k, i, s in order}
        self.per_turn = {}
        self.before, last = {}, {}
        for k, i, s in order:
            assert i == self.per_turn.get(k, 0), (k, i)
            self.per_turn[k] = i + 1
            self.before[k, i] = last.get(s)
            last[s] = (k, i)
        for key, prev in self.before.items():
            if prev is None:
                self.before[key] = (last[self.slot[key]][0], -1)

    def fill(self, eng, turn, kind, i):
        k, j = self.before[kind, i]
        for sem, n in self.release[k]:
            eng.wait_ge(sem, (turn * self.per_turn[k] + (j + 1)) * n)
        return self.tensors[self.slot[kind, i]]

    def filled(self, eng, turn, kind, i):
        eng.wait_ge(self.done[kind], turn * self.per_turn[kind] + i + 1)
        return self.tensors[self.slot[kind, i]]


def stand_alone(eng, waited):
    eng.sem_inc(waited, 1)


class Link:

    def __init__(self, eng, sem, per_turn=0):
        self.eng, self.sem, self.per_turn, self.turn, self.n = eng, sem, per_turn, 0, 0

    def __call__(self, ins):
        self.n += 1
        ins.then_inc(self.sem, 1)
        self.eng.wait_ge(self.sem, self.turn * self.per_turn + self.n)

    def done(self, ins):
        self.n += 1
        ins.then_inc(self.sem, 1)

    def wait(self):
        self.eng.wait_ge(self.sem, self.turn * self.per_turn + self.n)


def rsqrt(dve, link, y, v, a):
    link(dve.tensor_scalar(a.bitcast(U32), v.bitcast(U32), 1, None, ALU.logical_shift_right))
    link(dve.tensor_scalar(y.bitcast(I32), a.bitcast(I32), -1.0, float(MAGIC), ALU.mult, ALU.add))
    for _ in range(3):
        link(dve.scalar_tensor_tensor(out=a, in0=y, scalar=-0.5, in1=y, op0=ALU.mult, op1=ALU.mult))
        link(dve.tensor_tensor(a, a, v, ALU.mult))
        link(dve.scalar_tensor_tensor(out=y, in0=a, scalar=1.5, in1=y, op0=ALU.add, op1=ALU.mult))


def setup_block(nc, io, scratch, w):
    with ExitStack() as ctx:
        def sb(name, shape, dt=F32):
            return ctx.enter_context(nc.sbuf_tensor(name, shape, dt))

        def sem(name):
            return ctx.enter_context(nc.semaphore(name))

        c_t = sb("c_t", [P, KC, B])
        c_exp = sb("c_exp", [P, KC, B])
        c_silu = sb("c_silu", [P, KC, B])
        wmod = sb("wmod", [P, KC, 6 * D])
        raw = sb("raw", [P, 4, KC, D])
        mod = sb("mod", [B, 6 * D])
        sign = sb("sign", [B, D])
        mag = sb("mag", [B, D])
        ones = sb("ones", [B, D])
        zeros = sb("zeros", [B, D])
        mod_ps = ctx.enter_context(nc.psum_tensor("mod_ps", [P, 3, 512], F32))
        wt_ps = ctx.enter_context(nc.psum_tensor("wt_ps", [P, KC, 2, 512], F32))

        loaded = sem("loaded")
        loaded_w = sem("loaded_w")
        const_set = sem("const_set")
        exp_done = sem("exp_done")
        silu_done = sem("silu_done")
        mod_done = sem("mod_done")
        wt_done = sem("wt_done")
        hi_done = sem("hi_done")
        mod_ready = sem("mod_ready")
        stored = sem("stored")
        chain = sem("setup_chain")
        block = ctx.enter_context(nc.Block())

        @block.sync
        def _(sp):
            with nc.allow_non_contiguous_dma(reason="1024 words of c, transposed"):
                for k in range(KC):
                    sp.dma_start(c_t[:, k, :], io["c"].rearrange("b (k p) -> k p b", k=KC)[k]).then_inc(loaded, 16)
            sp.dma_start(wmod[:, :, :], io["wmod"].rearrange("(k p) n -> p k n", k=KC)).then_inc(loaded, 16)
            for i, name in enumerate(("wq", "wk", "wv", "wo")):
                sp.dma_start(raw[:, i, :, :], io[name].rearrange("(o p) n -> p o n", o=KC)).then_inc(loaded_w, 16)
            sp.dma_start(w["ident"][:, :], io["ident"]).then_inc(loaded_w, 16)
            for i, name in enumerate(("q_gamma", "k_gamma")):
                sp.dma_start(w["gamma"][:, i, :], io[name].unsqueeze(0).to_broadcast([P, HD])).then_inc(loaded_w, 16)
            sp.dma_start(w["bo"][:, :], io["bo"].unsqueeze(0).to_broadcast([P, D])).then_inc(loaded_w, 16)
            with nc.allow_non_contiguous_dma(reason="feature columns of the layer norm's gain and bias"):
                for i, name in enumerate(("ln_gamma", "ln_beta")):
                    sp.dma_start(w["ln"][:, i, :], io[name].rearrange("(k p) -> p k", k=KC)).then_inc(loaded_w, 16)
            sp.wait_ge(const_set, 2)
            for l in range(2):
                sp.dma_start(scratch["x"][l, :, 0, :], zeros[:, :]).then_inc(stored, 16)
            sp.dma_start(scratch["xa"][:, 0, :], zeros[:, :]).then_inc(stored, 16)
            sp.dma_start(scratch["gate"][0], ones[:, :]).then_inc(stored, 16)
            sp.wait_ge(mod_ready, 1)
            sp.dma_start(scratch["mod"], mod[:, :]).then_inc(stored, 16)
            sp.dma_start(scratch["gate"][1], mod[:, 5 * D:6 * D]).then_inc(stored, 16)
            sp.wait_ge(stored, 6 * 16)
            sp.wait_ge(loaded_w, 10 * 16)

        @block.scalar
        def _(act):
            act.wait_ge(loaded, 48)
            act.activation(c_exp[:, :, :], c_t[:, :, :], ACT.Exp, scale=-1.0).then_inc(exp_done, 1)
            for k in range(KC):
                for j in range(2):
                    act.wait_ge(wt_done, 2 * k + j + 1)
                    act.copy(w["hi"][:, k, 512 * j:512 * j + 512], wt_ps[:, k, j, :]).then_inc(hi_done, 1)

        @block.tensor
        def _(pe):
            pe.wait_ge(silu_done, 1)
            for n in range(3):
                for k in range(KC):
                    last = pe.matmul(mod_ps[0:B, n, :], c_silu[:, k, :], wmod[:, k, 512 * n:512 * n + 512],
                                     start=(k == 0), stop=(k == KC - 1))
            last.then_inc(mod_done, 1)
            pe.wait_ge(loaded_w, 10 * 16)
            for k in range(KC):
                for j in range(2):
                    for i in range(2):
                        for o in range(KC):
                            last = pe.transpose(wt_ps[:, k, j, D * i + P * o:D * i + P * o + P],
                                                raw[:, 2 * j + i, o, P * k:P * k + P], w["ident"][:, :])
                    last.then_inc(wt_done, 1)

        @block.vector
        def _(dve):
            link = Link(dve, chain)
            dve.memset(zeros[:, :], 0.0).then_inc(const_set, 1)
            dve.memset(ones[:, :], 1.0).then_inc(const_set, 1)
            dve.wait_ge(loaded, 48)
            dve.wait_ge(exp_done, 1)
            link(dve.tensor_scalar(c_exp[:, :, :], c_exp[:, :, :], 1.0, None, ALU.add))
            link(dve.reciprocal(c_exp[:, :, :], c_exp[:, :, :]))
            dve.tensor_tensor(c_silu[:, :, :], c_t[:, :, :], c_exp[:, :, :], ALU.mult).then_inc(silu_done, 1)
            dve.wait_ge(mod_done, 1)
            link(dve.tensor_copy(mod[:, :].rearrange("b (n m) -> b n m", n=3), mod_ps[0:B, :, :]))
            for i in (1, 4):
                link(dve.tensor_scalar(mod[:, D * i:D * i + D], mod[:, D * i:D * i + D], 1.0, None, ALU.add))
            for i in (2, 5):
                g = mod[:, D * i:D * i + D]
                link(dve.tensor_scalar(sign[:, :], g, 0.0, 2.0, ALU.is_ge, ALU.mult))
                link(dve.tensor_scalar(mag[:, :], g, -1.0, None, ALU.mult))
                link(dve.tensor_tensor(mag[:, :], mag[:, :], g, ALU.max))
                link(dve.tensor_scalar(mag[:, :], mag[:, :], 0.25, None, ALU.max))
                last = dve.scalar_tensor_tensor(out=g, in0=sign[:, :], scalar=-1.0, in1=mag[:, :],
                                                op0=ALU.add, op1=ALU.mult)
                if i == 2:
                    link(last)
            last.then_inc(mod_ready, 1)
            for i in range(2 * KC):
                dve.wait_ge(hi_done, i + 1)
                k, j = i // 2, i % 2
                dve.tensor_tensor(w["lo"][:, k, 512 * j:512 * j + 512], wt_ps[:, k, j, :],
                                  w["hi"][:, k, 512 * j:512 * j + 512].bitcast(F32), ALU.subtract)
            dve.wait_ge(loaded_w, 10 * 16)
            link(dve.tensor_scalar(w["gamma"][:, 0, :], w["gamma"][:, 0, :], float(HD) ** -0.5, None, ALU.mult))


def split3(pe, out, parts, wide, start=True, stop=True):
    last = None
    n = len(parts)
    for k, ((a_hi, a_lo), (b_hi, b_lo)) in enumerate(zip(parts, wide)):
        pe.matmul(out, a_hi, b_hi, start=(start and k == 0), stop=False)
        pe.matmul(out, a_hi, b_lo, start=False, stop=False)
        last = pe.matmul(out, a_lo, b_hi, start=False, stop=(stop and k == n - 1))
    return last


def attention_block(nc, io, scratch, w):
    with ExitStack() as ctx:
        def sb(name, shape, dt=F32):
            return ctx.enter_context(nc.sbuf_tensor(name, shape, dt))

        def sem(name):
            return ctx.enter_context(nc.semaphore(name))

        tensors = {s: ctx.enter_context(nc.psum_tensor(f"ps_{s}", [P, 2, 512], F32)) for s in ("A0", "A1", "M", "O")}
        order = []
        for i in range(NT + 1):
            if i < NT:
                order.append(("x_t", i, ("M", "O")[i % 2]))
            if i >= 1:
                order.append(("qkv", i - 1, ("A0", "A1")[(i - 1) % 2]))
        for i in range(NT):
            order.append(("qk_t", i, ("A0", "A1")[i % 2]))
            order.append(("kl_t", i, ("M", "O")[i % 2]))
        for i in range(NT):
            order.append(("max", i, ("M", "A0", "A1")[i % 3]))
        order.append(("m_t", 0, "M"))
        for h in range(GH):
            order.append(("out", h, "O"))
            for i in range(NT):
                order.append(("s_t", NT * h + i, ("A0", "A1")[i % 2]))
                if h + 1 < GH:
                    order.append(("max", NT * (h + 1) + i, "M"))
            if h + 1 < GH:
                order.append(("m_t", h + 1, "M"))
            order.append(("back", h, "M"))
        for i in range(NT):
            order.append(("y_t", i, ("M", "O")[i % 2]))
            order.append(("wo", i, ("A0", "A1")[i % 2]))

        x8 = sb("x8", [P, NT, D])
        h8 = sb("h8", [P, NT, D])
        mrow = sb("mrow", [P, 6, D])
        st = sb("st", [P, NT, 6])
        mv = sb("mv", [P, NT, 2])
        rs = sb("rs", [P, NT])
        var = sb("var", [P, NT])
        tmp = sb("tmp", [P, NT])
        x_f = sb("x_f", [P, 2, KC, P])
        x_hi = sb("x_hi", [P, 2, KC, P], F32R)
        x_lo = sb("x_lo", [P, 2, KC, P], F32R)
        qk8 = sb("qk8", [P, NT, 2 * GH * HD])
        sq = sb("sq", [P, 2, 2 * GH * HD])
        ss = sb("ss", [P, NT * 2 * GH])
        rr = sb("rr", [P, NT * 2 * GH])
        rt = sb("rt", [P, NT * 2 * GH])
        qn = sb("qn", [P, 2, 2, GH, HD])
        q_s = sb("q_s", [P, NT, GH, 3 * HD], F32R)
        k_s = sb("k_s", [P, 2, GH, 4 * HD], F32R)
        q1 = sb("q1", [P, GH, N], F32R)
        k1 = sb("k1", [P, GH, N], F32R)
        k2 = sb("k2", [P, GH, N], F32R)
        q2 = sb("q2", [P, 2, N], F32R)
        v1 = sb("v1", [P, NT, GH, HD + 1])
        pr = sb("pr", [P, 3, N])
        mx = sb("mx", [P, 2, NT])
        o_t = sb("o_t", [HD + 1, N])
        rc = sb("rc", [P, 2, 4])
        y_hi = sb("y_hi", [P, 2, KC, P], F32R)
        y_lo = sb("y_lo", [P, 2, KC, P], F32R)
        yb = sb("yb", [P, 2, D])
        one = sb("one", [P, GH * HD])

        kinds = ("x_t", "qkv", "qk_t", "kl_t", "max", "m_t", "s_t", "back", "y_t", "wo")
        done = {k: sem(f"{k}_done") for k in kinds}
        x_loaded = sem("x_loaded")
        preset = sem("preset")
        waited_sp = sem("waited_sp")
        waited_dve = sem("waited_dve")
        xn_ready = sem("xn_ready")
        xf_ready = sem("xf_ready")
        xt_ready = sem("xt_ready")
        qk_ready = sem("qk_ready")
        v_ready = sem("v_ready")
        sq_ready = sem("sq_ready")
        sq_used = sem("sq_used")
        qn_ready = sem("qn_ready")
        qg_ready = sem("qg_ready")
        hi_ready = sem("hi_ready")
        s_ready = sem("s_ready")
        q1_ready = sem("q1_ready")
        k1_ready = sem("k1_ready")
        k2_ready = sem("k2_ready")
        max_ready = sem("max_ready")
        m_ready = sem("m_ready")
        q2_ready = sem("q2_ready")
        p_ready = sem("p_ready")
        p_used = sem("p_used")
        ot_ready = sem("ot_ready")
        o8_ready = sem("o8_ready")
        yhi_ready = sem("yhi_ready")
        y_ready = sem("y_ready")
        yb_ready = sem("yb_ready")
        yg_ready = sem("yg_ready")
        x2_ready = sem("x2_ready")
        h0_ready = sem("h0_ready")
        st_x2 = sem("st_x2")
        st_h0 = sem("st_h0")
        chain = sem("chain")
        done["out"] = p_used
        slots = Slots(order, tensors, done, {
            "x_t": [(xf_ready, KC)], "qkv": [(v_ready, 1)], "qk_t": [(q1_ready, 1), (k1_ready, 1)],
            "kl_t": [(k2_ready, 1)], "max": [(max_ready, 1)], "m_t": [(q2_ready, 1)], "s_t": [(p_ready, 1)],
            "out": [(ot_ready, 1)], "back": [(o8_ready, 2)], "y_t": [(y_ready, 1)], "wo": [(yb_ready, 1)]})
        fill, filled = slots.fill, slots.filled
        block = ctx.enter_context(nc.Block())

        @block.sync
        def _(sp):
            with sp.Fori(0, B) as it:
                sp.dma_start(x8[:, :, :], io["x"][bass.ds(it, 1)].rearrange("a (t p) d -> p (a t) d", p=P)).then_inc(x_loaded, 16)
                sp.dma_start(mrow[:, :, :].rearrange("p s d -> p (s d)"),
                             scratch["mod"][bass.ds(it, 1), :].to_broadcast([P, 6 * D])).then_inc(x_loaded, 16)
                sp.wait_ge(x2_ready, NT * (it + 1))
                sp.dma_start(scratch["base"][bass.ds(it, 1)].rearrange("a (t p) d -> p (a t) d", p=P), x8[:, :, :]).then_inc(st_x2, 16)
                sp.wait_ge(h0_ready, it + 1)
                sp.dma_start(scratch["x"][0, bass.ds(it, 1), 1:N + 1, :].rearrange("a (t p) d -> p (a t) d", p=P), h8[:, :, :]).then_inc(st_h0, 16)
                sp.wait_ge(st_x2, 16 * (it + 1))
                sp.wait_ge(st_h0, 16 * (it + 1))
                stand_alone(sp, waited_sp)

        @block.gpsimd
        def _(pool):
            pool.memset(one[:, :], 0.0).then_inc(preset, 1)
            pool.memset(v1[:, :, :, HD:HD + 1], 1.0).then_inc(preset, 1)
            with pool.Fori(0, B) as it:
                for i in range(NT):
                    pool.wait_ge(qn_ready, it * NT + i + 1)
                    pool.tensor_tensor(qn[:, i % 2], qn[:, i % 2],
                                       w["gamma"][:, :, :].unsqueeze(2).to_broadcast([P, 2, GH, HD]),
                                       ALU.mult).then_inc(qg_ready, 1)
                for i in range(NT):
                    pool.wait_ge(yb_ready, it * NT + i + 1)
                    pool.tensor_tensor(yb[:, i % 2, :], yb[:, i % 2, :], mrow[:, 2, :], ALU.mult).then_inc(yg_ready, 1)
                    pool.wait_ge(yg_ready, it * NT + i + 1)
                    pool.tensor_tensor(x8[:, i, :], x8[:, i, :], yb[:, i % 2, :], ALU.add).then_inc(x2_ready, 1)

        def qkv_out(act, it, i):
            ps = filled(act, it, "qkv", i)
            act.copy(qk8[:, i, :], ps[:, 0, :]).then_inc(qk_ready, 1)
            act.copy(v1[:, i, :, 0:HD], ps[:, 1, 0:GH * HD].rearrange("p (h d) -> p h d", h=GH)).then_inc(v_ready, 1)
            act.wait_ge(qk_ready, it * NT + i + 1)
            if i >= 2:
                act.wait_ge(sq_used, it * NT + i - 1)
            act.activation(sq[:, i % 2, :], qk8[:, i, :], ACT.Square).then_inc(sq_ready, 1)

        def q1_out(act, it, i):
            ps = filled(act, it, "qk_t", i)
            act.copy(q1[:, :, P * i:P * i + P], ps[:, 0, :].rearrange("p (h n) -> p h n", h=GH)).then_inc(q1_ready, 1)

        @block.scalar
        def _(act):
            act.wait_ge(preset, 2)
            with act.Fori(0, B) as it:
                for i in range(NT):
                    ps = filled(act, it, "x_t", i)
                    if i >= 2:
                        act.wait_ge(xt_ready, it * NT + i - 1)
                    for k in range(KC):
                        act.activation(x_f[:, i % 2, k, :], ps[:, 0, P * k:P * k + P], ACT.Identity,
                                       scale=w["ln"][:, 0, k:k + 1], bias=w["ln"][:, 1, k:k + 1]).then_inc(xf_ready, 1)
                    if i >= 1:
                        qkv_out(act, it, i - 1)
                qkv_out(act, it, NT - 1)
                for i in range(NT):
                    act.wait_ge(qg_ready, it * NT + i + 1)
                    if i >= 2:
                        filled(act, it, "kl_t", i - 2)
                    act.copy(q_s[:, i, :, HD:2 * HD], qn[:, i % 2, 0, :, :]).then_inc(hi_ready, 1)
                    act.copy(k_s[:, i % 2, :, 0:2 * HD].rearrange("p h (r d) -> p h r d", r=2),
                             qn[:, i % 2, 1, :, :].unsqueeze(2).to_broadcast([P, GH, 2, HD])).then_inc(hi_ready, 1)
                    if i >= 1:
                        q1_out(act, it, i - 1)
                q1_out(act, it, NT - 1)
                for h in range(GH):
                    for i in range(NT):
                        n = h * NT + i
                        ps = filled(act, it, "s_t", n)
                        if n >= 3:
                            act.wait_ge(p_used, it * GH * NT + n - 2)
                        act.activation(pr[:, n % 3, :].rearrange("p (a b) -> p a b", a=2), ps[:, :, :],
                                       ACT.Exp).then_inc(p_ready, 1)
                for i in range(NT):
                    ps = filled(act, it, "y_t", i)
                    if i >= 2:
                        filled(act, it, "wo", i - 2)
                    act.copy(y_hi[:, i % 2, :, :].rearrange("p k n -> p (k n)"), ps[:, 0, 0:D]).then_inc(yhi_ready, 1)

        LINKS = (3 * (2 * NT + 1 + RSQRT_LINKS) + 2 * NT) + 3 + NT + (1 + RSQRT_LINKS) + GH

        @block.vector
        def _(dve):
            link = Link(dve, chain, LINKS)
            dve.wait_ge(preset, 1)
            for i in range(NT):
                link.done(dve.tensor_copy(q_s[:, i, :, 2 * HD:3 * HD], one[:, :].rearrange("p (h d) -> p h d", h=GH)))
            for i in range(2):
                link.done(dve.tensor_copy(k_s[:, i, :, 3 * HD:4 * HD], one[:, :].rearrange("p (h d) -> p h d", h=GH)))
            link.wait()
            link(dve.memset(one[:, 0:1], 1.0))
            for i in range(2):
                link.done(dve.tensor_copy(k_s[:, i, :, 3 * HD:3 * HD + 1], one[:, 0:1].unsqueeze(1).to_broadcast([P, GH, 1])))
            link.wait()
            base = link.n

            def row(r):
                return mrow[:, r, :].unsqueeze(1).to_broadcast([P, NT, D])

            def layer_norm(src, dst, last=None):
                for i in range(NT):
                    link.done(dve.bn_stats(st[:, i, :], src[:, i, :]))
                link.wait()
                stand_alone(dve, waited_dve)
                for i in range(NT):
                    link.done(dve.bn_aggr(mv[:, i, :], st[:, i, :]))
                link.wait()
                link(dve.tensor_scalar(var[:, :], mv[:, :, 1], LN_EPS, None, ALU.add))
                rsqrt(dve, link, rs[:, :], var[:, :], tmp[:, :])
                for i in range(NT):
                    ins = dve.tensor_scalar(dst[:, i, :], src[:, i, :], mv[:, i, 0:1], rs[:, i:i + 1],
                                            ALU.subtract, ALU.mult)
                    if last is None:
                        link.done(ins)
                    else:
                        ins.then_inc(last, 1)
                if last is None:
                    link.wait()

            with dve.Fori(0, B) as it:
                link.turn, link.n = it, base
                dve.wait_ge(x_loaded, 32 * (it + 1))
                layer_norm(x8, h8)
                link(dve.tensor_tensor(h8[:, :, :], h8[:, :, :], row(1), ALU.mult))
                link(dve.tensor_tensor(h8[:, :, :], h8[:, :, :], row(0), ALU.add))
                layer_norm(h8, h8, last=xn_ready)

                def square_sum(i):
                    dve.wait_ge(sq_ready, it * NT + i + 1)
                    dve.tensor_reduce(ss[:, 2 * GH * i:2 * GH * (i + 1)],
                                      sq[:, i % 2, :].rearrange("p (g d) -> p g d", d=HD), AX, ALU.add).then_inc(sq_used, 1)

                for i in range(NT):
                    dve.wait_ge(xf_ready, 2 * (it * NT + i) + 2)
                    if i >= 2:
                        filled(dve, it, "qkv", i - 2)
                    link(dve.tensor_copy(x_hi[:, i % 2], x_f[:, i % 2]))
                    dve.tensor_tensor(x_lo[:, i % 2], x_f[:, i % 2], x_hi[:, i % 2].bitcast(F32),
                                      ALU.subtract).then_inc(xt_ready, 1)
                    if i >= 1:
                        square_sum(i - 1)
                square_sum(NT - 1)
                dve.wait_ge(sq_used, (it + 1) * NT)
                link(dve.tensor_scalar(ss[:, :], ss[:, :], 1.0 / HD, RMS_EPS ** 2, ALU.mult, ALU.max))
                rsqrt(dve, link, rr[:, :], ss[:, :], rt[:, :])

                def k_out(i):
                    ps = filled(dve, it, "qk_t", i)
                    dve.tensor_copy(k1[:, :, P * i:P * i + P], ps[:, 1, :].rearrange("p (h n) -> p h n", h=GH)).then_inc(k1_ready, 1)
                    ps = filled(dve, it, "kl_t", i)
                    dve.tensor_copy(k2[:, :, P * i:P * i + P], ps[:, 0, :].rearrange("p (h n) -> p h n", h=GH)).then_inc(k2_ready, 1)

                for i in range(NT):
                    if i >= 2:
                        dve.wait_ge(s_ready, 2 * (it * NT + i - 1))
                    dve.tensor_tensor(qn[:, i % 2].rearrange("p a h d -> p (a h) d"),
                                      qk8[:, i, :].rearrange("p (g d) -> p g d", d=HD),
                                      rr[:, 2 * GH * i:2 * GH * (i + 1)].unsqueeze(2).to_broadcast([P, 2 * GH, HD]),
                                      ALU.mult).then_inc(qn_ready, 1)
                    dve.wait_ge(hi_ready, 2 * (it * NT + i) + 2)
                    dve.tensor_tensor(q_s[:, i, :, 0:HD], qn[:, i % 2, 0], q_s[:, i, :, HD:2 * HD].bitcast(F32),
                                      ALU.subtract).then_inc(s_ready, 1)
                    dve.tensor_tensor(k_s[:, i % 2, :, 2 * HD:3 * HD], qn[:, i % 2, 1],
                                      k_s[:, i % 2, :, 0:HD].bitcast(F32), ALU.subtract).then_inc(s_ready, 1)
                    if i >= 1:
                        k_out(i - 1)
                k_out(NT - 1)

                def row_max(h, i):
                    ps = filled(dve, it, "max", NT * h + i)
                    dve.tensor_reduce(mx[:, h % 2, i:i + 1], ps[:, :, :].rearrange("p a b -> p (a b)"), AX, ALU.max).then_inc(max_ready, 1)

                def minus_max(h):
                    dve.wait_ge(max_ready, (it * GH + h + 1) * NT)
                    dve.tensor_scalar(q_s[:, :, h, 2 * HD:2 * HD + 1], mx[:, h % 2, :].unsqueeze(2), -1.0, None,
                                      ALU.mult).then_inc(m_ready, 1)
                    ps = filled(dve, it, "m_t", h)
                    if h >= 2:
                        filled(dve, it, "s_t", NT * (h - 1) - 1)
                    dve.tensor_copy(q2[:, h % 2, :].rearrange("p (a b) -> p a b", a=2), ps[:, :, :]).then_inc(q2_ready, 1)

                for i in range(NT):
                    row_max(0, i)
                minus_max(0)
                for h in range(GH):
                    if h + 1 < GH:
                        for i in range(NT):
                            row_max(h + 1, i)
                        minus_max(h + 1)
                    dve.wait_ge(p_used, (it * GH + h + 1) * NT)
                    ps = slots.tensors["O"]
                    dve.tensor_copy(o_t[:, :].rearrange("p (a b) -> p a b", a=2), ps[0:HD + 1, :, :]).then_inc(ot_ready, 1)
                    ps = filled(dve, it, "back", h)
                    back = ps[:, :, :].rearrange("p a (i n) -> p a i n", n=P)
                    link(dve.reciprocal(rc[:, :, :], back[:, :, :, HD]))
                    for a in range(2):
                        dve.tensor_tensor(h8[:, 4 * a:4 * a + 4, HD * h:HD * h + HD], back[:, a, :, 0:HD],
                                          rc[:, a, :].unsqueeze(2).to_broadcast([P, 4, HD]),
                                          ALU.mult).then_inc(o8_ready, 1)

                for i in range(NT):
                    dve.wait_ge(yhi_ready, it * NT + i + 1)
                    dve.tensor_tensor(y_lo[:, i % 2].rearrange("p k n -> p (k n)"), slots.tensors[slots.slot["y_t", i]][:, 0, 0:D],
                                      y_hi[:, i % 2].rearrange("p k n -> p (k n)").bitcast(F32),
                                      ALU.subtract).then_inc(y_ready, 1)
                    ps = filled(dve, it, "wo", i)
                    if i >= 2:
                        dve.wait_ge(x2_ready, it * NT + i - 1)
                    dve.tensor_tensor(yb[:, i % 2, :], ps[:, 0, 0:D], w["bo"][:, :], ALU.add).then_inc(yb_ready, 1)
                dve.wait_ge(x2_ready, (it + 1) * NT)
                layer_norm(x8, h8)
                link(dve.tensor_tensor(h8[:, :, :], h8[:, :, :], row(4), ALU.mult))
                dve.tensor_tensor(h8[:, :, :], h8[:, :, :], row(3), ALU.add).then_inc(h0_ready, 1)
                assert link.n - base == LINKS, link.n - base

        @block.tensor
        def _(pe):
            pe.wait_ge(preset, 2)
            hi, lo, ident = w["hi"], w["lo"], w["ident"]
            with pe.Fori(0, B) as it:
                def x_transpose(i):
                    ps = fill(pe, it, "x_t", i)
                    pe.wait_ge(xn_ready, it * NT + i + 1)
                    for k in range(KC):
                        last = pe.transpose(ps[:, 0, P * k:P * k + P], h8[:, i, P * k:P * k + P], ident[:, :])
                    last.then_inc(done["x_t"], 1)

                def qkv(i):
                    ps = fill(pe, it, "qkv", i)
                    pe.wait_ge(xt_ready, it * NT + i + 1)
                    a = [(x_hi[:, i % 2, k, :], x_lo[:, i % 2, k, :]) for k in range(KC)]
                    split3(pe, ps[:, 0, :], a, [(hi[:, k, 0:512], lo[:, k, 0:512]) for k in range(KC)])
                    split3(pe, ps[:, 1, 0:D], a, [(hi[:, k, 512:768], lo[:, k, 512:768]) for k in range(KC)]).then_inc(done["qkv"], 1)

                for i in range(NT + 1):
                    if i < NT:
                        x_transpose(i)
                    if i >= 1:
                        qkv(i - 1)
                for i in range(NT):
                    ps = fill(pe, it, "qk_t", i)
                    pe.wait_ge(s_ready, 2 * (it * NT + i) + 2)
                    for h in range(GH):
                        pe.transpose(ps[:, 0, P * h:P * h + P], q_s[:, i, h, 0:P].bitcast(F32), ident[:, :])
                    for h in range(GH):
                        last = pe.transpose(ps[:, 1, P * h:P * h + P], k_s[:, i % 2, h, 0:P].bitcast(F32), ident[:, :])
                    last.then_inc(done["qk_t"], 1)
                    ps = fill(pe, it, "kl_t", i)
                    for h in range(GH):
                        last = pe.transpose(ps[:, 0, P * h:P * h + P], k_s[:, i % 2, h, P:2 * P].bitcast(F32), ident[:, :])
                    last.then_inc(done["kl_t"], 1)

                def maxima(h, i):
                    ps = fill(pe, it, "max", NT * h + i)
                    for a in range(2):
                        last = pe.matmul(ps[:, a, :], q1[:, h, P * i:P * i + P], k1[:, h, HALF * a:HALF * a + HALF],
                                         start=True, stop=True)
                    last.then_inc(done["max"], 1)

                def max_transpose(h):
                    ps = fill(pe, it, "m_t", h)
                    pe.wait_ge(m_ready, it * GH + h + 1)
                    for i in range(NT):
                        last = pe.transpose(ps[:, i // 4, P * (i % 4):P * (i % 4) + P],
                                            q_s[:, i, h, HD:3 * HD].bitcast(F32), ident[:, :])
                    last.then_inc(done["m_t"], 1)

                for ready in (q1_ready, k1_ready, k2_ready):
                    pe.wait_ge(ready, NT * (it + 1))
                for i in range(NT):
                    maxima(0, i)
                max_transpose(0)

                def values(h, i):
                    n = h * NT + i
                    pe.wait_ge(p_ready, it * GH * NT + n + 1)
                    for a in range(2):
                        last = pe.matmul(slots.tensors["O"][0:HD + 1, a, :], v1[:, i, h, :], pr[:, n % 3, HALF * a:HALF * a + HALF],
                                         start=(i == 0), stop=(i == NT - 1))
                    last.then_inc(p_used, 1)

                for h in range(GH):
                    pe.wait_ge(q2_ready, it * GH + h + 1)
                    fill(pe, it, "out", h)
                    for i in range(NT):
                        ps = fill(pe, it, "s_t", NT * h + i)
                        for a in range(2):
                            cols = slice(HALF * a, HALF * a + HALF)
                            pe.matmul(ps[:, a, :], k1[:, h, P * i:P * i + P], q1[:, h, cols], start=True, stop=False)
                            last = pe.matmul(ps[:, a, :], k2[:, h, P * i:P * i + P], q2[:, h % 2, cols], start=False, stop=True)
                        last.then_inc(done["s_t"], 1)
                        if h + 1 < GH:
                            maxima(h + 1, i)
                        if i >= 1:
                            values(h, i - 1)
                    values(h, NT - 1)
                    if h + 1 < GH:
                        max_transpose(h + 1)
                    ps = fill(pe, it, "back", h)
                    pe.wait_ge(ot_ready, it * GH + h + 1)
                    for i in range(NT):
                        last = pe.transpose(ps[:, i // 4, P * (i % 4):P * (i % 4) + HD + 1],
                                            o_t[:, P * i:P * i + P], ident[0:HD + 1, 0:HD + 1])
                    last.then_inc(done["back"], 1)

                pe.wait_ge(o8_ready, 2 * GH * (it + 1))

                def y_transpose(i):
                    ps = fill(pe, it, "y_t", i)
                    for k in range(KC):
                        last = pe.transpose(ps[:, 0, P * k:P * k + P], h8[:, i, P * k:P * k + P], ident[:, :])
                    last.then_inc(done["y_t"], 1)

                for i in range(NT):
                    y_transpose(i)
                    ps = fill(pe, it, "wo", i)
                    pe.wait_ge(y_ready, it * NT + i + 1)
                    a = [(y_hi[:, i % 2, k, :], y_lo[:, i % 2, k, :]) for k in range(KC)]
                    split3(pe, ps[:, 0, 0:D], a, [(hi[:, k, 768:1024], lo[:, k, 768:1024]) for k in range(KC)]).then_inc(done["wo"], 1)


LH = 8
INNER = LH * HD
PAIRS = LH // 2
HID = D * 4 * 2 // 3
NL = 2
TURNS = NT // 2
NC = -(-HID // P)
CS = [HID // NC + (j < HID % NC) for j in range(NC)]
CO = [sum(CS[:j]) for j in range(NC)]
BIG = -1e30
NORM_EPS = 1e-12
QK_SCALE = 8.0


def layers_block(nc, io, scratch, out, ident):
    with ExitStack() as ctx:
        def sb(name, shape, dt=F32):
            return ctx.enter_context(nc.sbuf_tensor(f"l_{name}", shape, dt))

        def sem(name):
            return ctx.enter_context(nc.semaphore(f"l_{name}"))

        wqkv = [sb(f"wqkv_{s}", [P, KC, 3 * INNER], F32R) for s in ("hi", "lo")]
        wo = [sb(f"wo_{s}", [P, PAIRS, D], F32R) for s in ("hi", "lo")]
        w1 = [sb(f"w1_{s}", [P, KC, 2 * HID], F32R) for s in ("hi", "lo")]
        w2 = [sb(f"w2_{s}", [P, NC, D], F32R) for s in ("hi", "lo")]
        scales = sb("scales", [P, 4, HD])
        gb = sb("gb", [P, 2, KC])
        b1 = sb("b1", [P, 2 * NC])
        b2 = sb("b2", [P, D])
        gate = sb("gate", [P, B, D])
        flag = sb("flag", [P, 1])
        xs = sb("xs", [P, 2, B, 3, P])
        h_hi = sb("h_hi", [P, 2, KC, P], F32R)
        h_lo = sb("h_lo", [P, 2, KC, P], F32R)
        qk = sb("qk", [P, 2, 2 * LH, HD])
        t1 = sb("t1", [P, 2 * LH, HD])
        t2 = sb("t2", [P, 2 * LH, HD])
        ss = sb("ss", [P, 2 * LH])
        ra = sb("ra", [P, 2 * LH])
        rn = sb("rn", [P, B, 2 * LH])
        tab_in = sb("tab_in", [P, 4, HD])
        tab = sb("tab", [P, 2, 4, HD])
        mask = sb("mask", [P, 2, 2 * P])
        qt = sb("qt", [P, 2, LH, P])
        kt = sb("kt", [P, B, PAIRS, 2, P])
        vt = sb("vt", [P, B, 2, INNER])
        sm = sb("sm", [P, 4, 2, 2 * P])
        pt = sb("pt", [P, 2, 4, P])
        mx = sb("mx2", [P, 4, 2])
        nb = sb("nb", [P, 4, 2])
        rsum = sb("rsum", [P, 4, 2])
        rinv = sb("rinv", [P, 4, 2])
        o_hi = sb("o_hi", [P, 2, PAIRS, P], F32R)
        o_lo = sb("o_lo", [P, 2, PAIRS, P], F32R)
        st = sb("st2", [P, 6])
        mv = sb("mv2", [P, 2])
        rs = sb("rs2", [P, 1])
        var = sb("var2", [P, 1])
        tmp = sb("tmp2", [P, 1])
        xn = sb("xn", [P, 2, D])
        f_hi = sb("f_hi", [P, KC, B * P], F32R)
        f_lo = sb("f_lo", [P, KC, B * P], F32R)
        ge = sb("ge", [P, 2, B * P])
        up = sb("up", [P, 2, B * P])
        u_hi = sb("u_hi", [P, 2, B * P], F32R)
        u_lo = sb("u_lo", [P, 2, B * P], F32R)
        yb = sb("yb2", [P, B, D])
        base = sb("base", [P, B, D])
        stage = [qk[:, :, :, :].rearrange("p a h d -> p (a h d)"), sm[:, :, :, :].rearrange("p a b n -> p (a b n)")]

        banks = {s: ctx.enter_context(nc.psum_tensor(f"bank_{s}", [P, 512], F32))
                 for s in ("P0", "P1", "T0", "T1", "S0", "S1", "O0", "O1")}

        order, count = [], {}
        rings = {"T": 0, "P": 0}

        def use(kind, ring):
            i = count.get(kind, 0)
            count[kind] = i + 1
            if ring in rings:
                slot = f"{ring}{rings[ring] % 2}"
                rings[ring] += 1
            else:
                slot = ring
            order.append((kind, i, slot))

        LAG = 3
        for p in range(2):
            def a_h():
                use("h_t", "T")

            def a_qkv():
                use("qk", "P")
                use("qk", "P")
                use("v", "P")

            def a_t():
                use("q_t", "T")
                use("k_t", "T")

            a_h(), a_h(), a_qkv(), a_qkv(), a_h(), a_t()
            for r in range(B * PAIRS + 5):
                b, j = divmod(r, PAIRS)
                if b < B:
                    use("s", f"S{r % 2}")
                if b + 2 < B and j == 0:
                    a_qkv()
                if 0 <= r - LAG < B * PAIRS:
                    use("p_t", "T")
                    if (r - LAG) % PAIRS == 0:
                        use("o", f"O{(r - LAG) // PAIRS % 2}")
                if b + 1 < B and j == 2:
                    a_t()
                if b + 3 < B and j == 3:
                    a_h()
                if r >= 8 and j == 0:
                    use("wo", "P")
            for b in range(B):
                use("x_t", "T")
            for j in range(NC):
                use("a", ("P0", "S0")[j % 2])
                use("g", ("P1", "S1")[j % 2])
                if j == 1:
                    use("y", "O0")
                    use("y", "O1")

        done = {k: sem(f"{k}_done2") for k in count if k not in ("o", "y")}
        pv_done = sem("pv_done")
        w2_done = sem("w2_done")
        done["o"], done["y"] = pv_done, w2_done
        w_loaded = [sem("w_loaded0"), sem("w_loaded1")]
        par_loaded = sem("par_loaded")
        w_hi = sem("w_hi")
        w_lo = sem("w_lo")
        bias_done = sem("bias_done")
        waited_pool, waited_dve, waited_pe, waited_sp = (sem(f"waited_{e}") for e in ("pool", "dve", "pe", "sp"))
        preset = sem("preset2")
        xs_loaded = [[sem(f"xs_loaded{p}{b}") for b in range(B)] for p in range(2)]
        base_loaded = [sem(f"base_loaded{b}") for b in range(B)]
        mask_loaded = sem("mask_loaded")
        tab_loaded = sem("tab_loaded")
        tab_ready = sem("tab_ready")
        hhi_ready = sem("hhi_ready")
        h_ready = sem("h_ready")
        qk_ready = sem("qk_ready2")
        v_ready = sem("v_ready2")
        sq_ready = sem("sq_ready2")
        sq_used = sem("sq_used2")
        t1_ready = sem("t1_ready")
        t2_ready = sem("t2_ready")
        rot_ready = sem("rot_ready")
        qt_ready = sem("qt_ready")
        kt_ready = sem("kt_ready")
        sm_ready = sem("sm_ready")
        nb_ready = sem("nb_ready")
        ex_ready = sem("ex_ready")
        ri_ready = sem("ri_ready")
        pn_ready = sem("pn_ready")
        pt_ready = sem("pt_ready")
        ohi_ready = sem("ohi_ready")
        o_ready = sem("o_ready")
        x1_ready = sem("x1_ready")
        x1_stored = sem("x1_stored")
        sh_loaded = [sem(f"sh_loaded{b}") for b in range(B)]
        xn_ready = [sem(f"xn_ready{p}") for p in range(2)]
        xb_ready = [sem(f"xb_ready{p}") for p in range(2)]
        fhi_ready = sem("fhi_ready")
        f_ready = sem("f_ready")
        ge_ready = sem("ge_ready")
        up_ready = sem("up_ready")
        uhi_ready = sem("uhi_ready")
        u_ready = sem("u_ready")
        y_ready = sem("y_ready2")
        gy_ready = sem("gy_ready")
        y2_ready = sem("y2_ready")
        y_stored = [sem(f"y_stored{b}") for b in range(B)]
        o_stored = [sem(f"o_stored{b}") for b in range(B)]
        chain_w = sem("chain_w")
        chain = sem("chain2")
        slots = Slots(order, banks, done, {
            "h_t": [(h_ready, 1)], "qk": [(qk_ready, 1)], "v": [(v_ready, 1)], "q_t": [(qt_ready, 2)],
            "k_t": [(kt_ready, 1)], "s": [(sm_ready, 2)], "p_t": [(pt_ready, 1)], "o": [(o_ready, 1)],
            "wo": [(x1_ready, 1)], "x_t": [(f_ready, 1)], "a": [(up_ready, 1)], "g": [(ge_ready, 1)],
            "y": [(y_ready, 2)]})
        fill, filled = slots.fill, slots.filled
        STAGED = 6
        block = ctx.enter_context(nc.Block())

        @block.sync
        def _(sp):
            for b in range(B):
                sp.sem_inc(y_stored[b], 16 * NT)
            with sp.Fori(0, NL) as l:
                def row(name):
                    return io[name][bass.ds(l, 1)]

                for b in range(B):
                    sp.wait_ge(y_stored[b], 16 * NT * (l + 1))
                for i, (name, cut) in enumerate((("q_scale", 0), ("k_scale", 0))):
                    sp.dma_start(scales[:, 2 * i, :], row(name).to_broadcast([P, HD])).then_inc(par_loaded, 16)
                    sp.dma_start(scales[:, 2 * i + 1, 0:HD // 2], row(name)[:, HD // 2:HD].to_broadcast([P, HD // 2])).then_inc(par_loaded, 16)
                    sp.dma_start(scales[:, 2 * i + 1, HD // 2:HD], row(name)[:, 0:HD // 2].to_broadcast([P, HD // 2])).then_inc(par_loaded, 16)
                with nc.allow_non_contiguous_dma(reason="parameters by feature, a column each"):
                    for i, name in enumerate(("lg", "lb")):
                        sp.dma_start(gb[:, i, :], row(name).rearrange("a (k p) -> p (a k)", k=KC)).then_inc(par_loaded, 16)
                    for g in range(2):
                        for j in range(NC):
                            sp.dma_start(b1[0:CS[j], NC * g + j:NC * g + j + 1],
                                         row("b1")[:, HID * g + CO[j]:HID * g + CO[j] + CS[j]].rearrange("a p -> p a")).then_inc(par_loaded, 16)
                sp.dma_start(b2[:, :], row("b2").to_broadcast([P, D])).then_inc(par_loaded, 16)
                sp.dma_start(flag[:, :], row("flags").to_broadcast([P, 1])).then_inc(par_loaded, 16)
                sp.dma_start(gate[:, :, :].rearrange("p b d -> p (b d)"),
                             scratch["gate"][bass.ds(l, 1)].rearrange("a b d -> a (b d)").to_broadcast([P, B * D])).then_inc(par_loaded, 16)
                wq_v = row("wqkv").rearrange("a (k p) n -> p (a k) n", k=KC)
                w1_v = row("w1").rearrange("a (k p) n -> p (a k) n", k=KC)
                for i in range(STAGED):
                    if i >= 2:
                        sp.wait_ge(w_lo, STAGED * l + i - 1)
                    s = stage[i % 2]
                    if i < 2:
                        pairs = [(s[:, 0:3 * INNER], wq_v[:, i, :])]
                    elif i == 2:
                        pairs = [(s[:, 0:PAIRS * D].rearrange("p (c n) -> p c n", c=PAIRS),
                                  row("f_wo").rearrange("a (c p) n -> p (a c) n", c=PAIRS))]
                    elif i < 5:
                        pairs = [(s[:, 0:2 * HID], w1_v[:, i - 3, :])]
                    else:
                        n = CS.count(CS[0])
                        v = s[:, 0:NC * D].rearrange("p (c n) -> p c n", c=NC)
                        pairs = [(v[0:CS[0], 0:n, :], row("w2")[:, 0:CO[n], :].rearrange("a (c p) n -> p (a c) n", c=n)),
                                 (v[0:CS[-1], n:NC, :], row("w2")[:, CO[n]:HID, :].rearrange("a (c p) n -> p (a c) n", c=NC - n))]
                    for dst, src in pairs:
                        sp.dma_start(dst, src).then_inc(w_loaded[i % 2], 16)

                with sp.Fori(0, TURNS) as tp:
                    u = l * TURNS + tp
                    for p in range(2):
                        t = tp * 2 + p
                        step = u * 2 + p
                        sp.wait_ge(tab_ready, step)
                        sp.dma_start(tab_in[:, :, :], io["rope"][bass.ds(t, 1)].rearrange("a p c d -> p (a c) d")).then_inc(tab_loaded, 16)
                        if p == 0:
                            sp.wait_ge(sm_ready, u * 2 * 2 * B * PAIRS)
                            sp.dma_start(mask[:, :, :], io["mask"][bass.ds(tp, 1)].rearrange("a p c n -> p (a c) n")).then_inc(mask_loaded, 16)
                        for b in range(B):
                            sp.wait_ge(xn_ready[p], B * u)
                            sp.wait_ge(xb_ready[p], B * u)
                            sp.wait_ge(y_stored[b], 16 * (step + 1))
                            src = scratch["x"][bass.ds(l, 1), b]
                            sp.dma_start(xs[:, p, b, 0:3:2, :],
                                         src[:, bass.ds(t * P + 1, P), :].rearrange("a p (c n) -> p (a c) n", c=2)).then_inc(xs_loaded[p][b], 16)
                            sp.dma_start(xs[:, p, b, 1, :],
                                         src[:, bass.ds(t * P, P), P:D].rearrange("a p n -> p (a n)")).then_inc(xs_loaded[p][b], 16)
                            sp.wait_ge(y2_ready, B * step)
                            stand_alone(sp, waited_sp)
                            sp.dma_start(base[:, b, :], scratch["base"][b, bass.ds(t * P, P), :]).then_inc(base_loaded[b], 16)
                        for b in range(B):
                            sp.wait_ge(x1_ready, B * step + b + 1)
                            stand_alone(sp, waited_sp)
                            sp.dma_start(scratch["xa"][b, bass.ds(t * P + 1, P), :].rearrange("p (c n) -> p c n", c=2),
                                         xs[:, p, b, 0:3:2, :]).then_inc(x1_stored, 16)
                            sp.wait_ge(x1_stored, 16 * (B * step + b + 1))
                            sp.dma_start(xs[:, p, b, 1, :], scratch["xa"][b, bass.ds(t * P, P), P:D]).then_inc(sh_loaded[b], 16)
                        for b in range(B):
                            sp.wait_ge(y2_ready, B * step + b + 1)
                            stand_alone(sp, waited_sp)
                            sp.dma_start(scratch["x"][bass.ds(l + 1, 1), b, bass.ds(t * P + 1, P), :].rearrange("a p n -> p (a n)"),
                                         yb[:, b, :]).then_inc(y_stored[b], 16)
                            sp.wait_ge(o_stored[b], 16 * step)
                            sp.dma_start(out[b, bass.ds(t * P, P), :], yb[:, b, :]).then_inc(o_stored[b], 16)
            for b in range(B):
                sp.wait_ge(y_stored[b], 16 * NT * (NL + 1))
                sp.wait_ge(o_stored[b], 16 * NT * NL)

        @block.gpsimd
        def _(pool):
            pool.memset(qt[:, :, :, :], 0.0).then_inc(preset, 1)
            pool.memset(kt[:, :, :, :, :], 0.0).then_inc(preset, 1)
            pool.memset(vt[:, :, :, :], 0.0).then_inc(preset, 1)
            PAR = 16 * (6 + 2 + 2 * NC + 3)
            with pool.Fori(0, NL) as l:
                pool.wait_ge(par_loaded, PAR * (l + 1))
                stand_alone(pool, waited_pool)
                with pool.Fori(0, TURNS) as tp:
                    u = l * TURNS + tp
                    for p in range(2):
                        def n_of(b):
                            return B * p + b

                        pool.wait_ge(tab_loaded, 16 * (2 * u + p + 1))
                        pool.wait_ge(t1_ready, u * 2 * B)
                        pool.tensor_tensor(tab[:, p], tab_in[:, :, :], scales[:, :, :], ALU.mult).then_inc(tab_ready, 1)

                        def rotate(b):
                            n = u * 2 * B + n_of(b)
                            pool.wait_ge(tab_ready, 2 * u + p + 1)
                            pool.wait_ge(sq_used, n + 1)
                            pool.wait_ge(qk_ready, 2 * n + 2)
                            src = qk[:, b % 2].rearrange("p (a h) d -> p a h d", a=2)
                            dst = t2[:, :, :].rearrange("p (a h) d -> p a h d", a=2)
                            H2 = HD // 2
                            for lo, hi in ((0, H2), (H2, 0)):
                                for a in range(2):
                                    pool.tensor_tensor(dst[:, a, :, lo:lo + H2], src[:, a, :, hi:hi + H2],
                                                       tab[:, p, 2 * a + 1, lo:lo + H2].unsqueeze(1).to_broadcast([P, LH, H2]),
                                                       ALU.mult).then_inc(t2_ready, 1)

                        def probabilities(r):
                            n = (2 * u + p) * B * PAIRS + r
                            pool.wait_ge(ri_ready, n + 1)
                            pool.tensor_tensor(sm[:, r % 4], sm[:, r % 4],
                                               rinv[:, r % 4, :].unsqueeze(2).to_broadcast([P, 2, 2 * P]),
                                               ALU.mult).then_inc(pn_ready, 1)

                        rotate(0)
                        rotate(1)
                        for r in range(B * PAIRS + 1):
                            b, j = divmod(r, PAIRS)
                            if r >= 1:
                                probabilities(r - 1)
                            if b + 2 < B and j == 3:
                                rotate(b + 2)
                        for b in range(B):
                            pool.wait_ge(x1_ready, u * 2 * B + n_of(b) + 1)
                            pool.wait_ge(y_stored[b], 16 * (NT + 2 * u + p))
                            pool.wait_ge(o_stored[b], 16 * (2 * u + p))
                            pool.tensor_tensor(yb[:, b, :].rearrange("p (c n) -> p c n", c=2), xs[:, p, b, 0:3:2, :],
                                               b2[:, :].rearrange("p (c n) -> p c n", c=2), ALU.add).then_inc(xb_ready[p], 1)
                        for j in range(NC):
                            m = (2 * u + p) * NC + j
                            pool.wait_ge(uhi_ready, m + 1)
                            pool.tensor_tensor(u_lo[0:CS[j], j % 2, :], up[0:CS[j], j % 2, :],
                                               u_hi[0:CS[j], j % 2, :].bitcast(F32), ALU.subtract).then_inc(u_ready, 1)
                        for b in range(B):
                            pool.wait_ge(y_ready, u * 2 * B + n_of(b) + 1)
                            pool.tensor_tensor(yb[:, b, :], yb[:, b, :], gate[:, b, :], ALU.mult).then_inc(gy_ready, 1)

        @block.scalar
        def _(act):
            PAR = 16 * (6 + 2 + 2 * NC + 3)
            with act.Fori(0, NL) as l:
                act.wait_ge(par_loaded, PAR * (l + 1))
                loads = [0, 0]
                per_stage = [3, 4]
                for i in range(STAGED):
                    loads[i % 2] += 2 if i == 5 else 1
                    act.wait_ge(w_loaded[i % 2], 16 * (per_stage[i % 2] * l + loads[i % 2]))
                    s = stage[i % 2]
                    if i < 2:
                        act.copy(wqkv[0][:, i, :], s[:, 0:3 * INNER]).then_inc(w_hi, 1)
                    elif i == 2:
                        act.copy(wo[0][:, :, :].rearrange("p c n -> p (c n)"), s[:, 0:PAIRS * D]).then_inc(w_hi, 1)
                    elif i < 5:
                        act.activation(w1[0][:, i - 3, :], s[:, 0:2 * HID], ACT.Copy, scale=gb[:, 0, i - 3:i - 2]).then_inc(w_hi, 1)
                    else:
                        n = CS.count(CS[0])
                        v = s[:, 0:NC * D].rearrange("p (c n) -> p c n", c=NC)
                        act.copy(w2[0][0:CS[0], 0:n, :], v[0:CS[0], 0:n, :]).then_inc(w_hi, 1)
                        act.copy(w2[0][0:CS[-1], n:NC, :], v[0:CS[-1], n:NC, :]).then_inc(w_hi, 1)
                with act.Fori(0, TURNS) as tp:
                    u = l * TURNS + tp
                    for p in range(2):
                        base_n = u * 2 * B + B * p

                        def h_out(b):
                            ps = filled(act, u, "h_t", B * p + b)
                            if B * p + b >= 2:
                                filled(act, u, "v", B * p + b - 2)
                            act.copy(h_hi[:, b % 2].rearrange("p k n -> p (k n)"), ps[:, 0:D]).then_inc(hhi_ready, 1)

                        def qkv_out(b):
                            n = base_n + b
                            if B * p + b >= 2:
                                filled(act, u, "k_t", B * p + b - 2)
                            for a in range(2):
                                ps = filled(act, u, "qk", 2 * (B * p + b) + a)
                                act.copy(qk[:, b % 2, LH * a:LH * a + LH, :].rearrange("p h d -> p (h d)"), ps[:, :]).then_inc(qk_ready, 1)
                            act.wait_ge(qk_ready, 2 * n + 2)
                            act.wait_ge(rot_ready, n)
                            act.activation(t2[:, :, :], qk[:, b % 2], ACT.Square).then_inc(sq_ready, 1)
                            ps = filled(act, u, "v", B * p + b)
                            act.copy(vt[:, b, p, :], ps[:, :]).then_inc(v_ready, 1)

                        def k_out(b):
                            ps = filled(act, u, "k_t", B * p + b)
                            act.copy(kt[:, b, :, p, :], ps[:, :].rearrange("p (c n) -> p c n", c=PAIRS)).then_inc(kt_ready, 1)

                        def exps(r):
                            n = (2 * u + p) * B * PAIRS + r
                            act.wait_ge(nb_ready, n + 1)
                            for e in range(2):
                                act.activation(sm[:, r % 4, e, :], sm[:, r % 4, e, :], ACT.Exp, bias=nb[:, r % 4, e:e + 1],
                                               scale=rn[:, r // PAIRS, 2 * (r % PAIRS) + e:2 * (r % PAIRS) + e + 1],
                                               accum_out=rsum[:, r % 4, e:e + 1]).then_inc(ex_ready, 1)

                        def pt_out(r):
                            ps = filled(act, u, "p_t", B * PAIRS * p + r)
                            n = (2 * u + p) * B * PAIRS + r
                            if B * PAIRS * p + r >= 2:
                                act.wait_ge(pv_done, n - 1)
                            act.copy(pt[:, r % 2].rearrange("p c n -> p (c n)"), ps[:, :]).then_inc(pt_ready, 1)

                        def o_out(b):
                            act.wait_ge(pv_done, (base_n + b + 1) * PAIRS)
                            if B * p + b >= 2:
                                filled(act, u, "wo", B * p + b - 2)
                            act.copy(o_hi[:, b % 2].rearrange("p c n -> p (c n)"), banks[f"O{b % 2}"][:, :]).then_inc(ohi_ready, 1)

                        h_out(0), h_out(1), qkv_out(0), qkv_out(1), h_out(2), k_out(0)
                        for r in range(B * PAIRS + 5):
                            b, j = divmod(r, PAIRS)
                            if b < B:
                                exps(r)
                            if b + 2 < B and j == 0:
                                qkv_out(b + 2)
                            if 0 <= r - LAG < B * PAIRS:
                                pt_out(r - LAG)
                            if b + 1 < B and j == 2:
                                k_out(b + 1)
                            if b + 3 < B and j == 3:
                                h_out(b + 3)
                            if r >= 7 and j == 3:
                                o_out(b - 1)
                        for b in range(B):
                            ps = filled(act, u, "x_t", B * p + b)
                            act.copy(f_hi[:, :, P * b:P * b + P], ps[:, 0:D].rearrange("p (k n) -> p k n", k=KC)).then_inc(fhi_ready, 1)
                        for j in range(NC + 1):
                            m = (2 * u + p) * NC + j
                            if j < NC:
                                ps = filled(act, u, "g", NC * p + j)
                                if NC * p + j >= 2:
                                    act.wait_ge(up_ready, m - 1)
                                act.activation(ge[0:CS[j], j % 2, :], ps[0:CS[j], :], ACT.Gelu,
                                               bias=b1[0:CS[j], NC + j:NC + j + 1]).then_inc(ge_ready, 1)
                            if j >= 1:
                                k = j - 1
                                act.wait_ge(up_ready, m)
                                if NC * p + k >= 2:
                                    act.wait_ge(w2_done, B * (m - 2))
                                act.copy(u_hi[0:CS[k], k % 2, :], up[0:CS[k], k % 2, :]).then_inc(uhi_ready, 1)

        LINKS_W = 1 + 2 * KC
        LINKS = 2 * B * ((3 + RSQRT_LINKS) + 2 + (3 + RSQRT_LINKS))

        @block.vector
        def _(dve):
            PAR = 16 * (6 + 2 + 2 * NC + 3)
            dve.wait_ge(preset, 3)
            link_w, link = Link(dve, chain_w, LINKS_W), Link(dve, chain, LINKS)
            with dve.Fori(0, NL) as l:
                link_w.turn, link_w.n = l, 0
                dve.wait_ge(par_loaded, PAR * (l + 1))
                for i in range(STAGED):
                    dve.wait_ge(w_hi, (STAGED + 1) * l + i + 1 + (i == 5))
                    s = stage[i % 2]
                    if i < 2:
                        dve.tensor_tensor(wqkv[1][:, i, :], s[:, 0:3 * INNER], wqkv[0][:, i, :].bitcast(F32),
                                          ALU.subtract).then_inc(w_lo, 1)
                    elif i == 2:
                        dve.tensor_tensor(wo[1][:, :, :].rearrange("p c n -> p (c n)"), s[:, 0:PAIRS * D],
                                          wo[0][:, :, :].rearrange("p c n -> p (c n)").bitcast(F32), ALU.subtract).then_inc(w_lo, 1)
                    elif i < 5:
                        dve.wait_ge(bias_done, KC * l + i - 2)
                        dve.scalar_tensor_tensor(out=w1[1][:, i - 3, :], in0=s[:, 0:2 * HID], scalar=gb[:, 0, i - 3:i - 2],
                                                 in1=w1[0][:, i - 3, :].bitcast(F32), op0=ALU.mult, op1=ALU.subtract).then_inc(w_lo, 1)
                    else:
                        n = CS.count(CS[0])
                        v = s[:, 0:NC * D].rearrange("p (c n) -> p c n", c=NC)
                        link_w(dve.tensor_tensor(w2[1][0:CS[0], 0:n, :], v[0:CS[0], 0:n, :], w2[0][0:CS[0], 0:n, :].bitcast(F32), ALU.subtract))
                        dve.tensor_tensor(w2[1][0:CS[-1], n:NC, :], v[0:CS[-1], n:NC, :], w2[0][0:CS[-1], n:NC, :].bitcast(F32),
                                          ALU.subtract).then_inc(w_lo, 1)
                n = CS.count(CS[0])
                b1_v = b1[:, :].rearrange("p (g c) -> p g c", g=2)
                for rows, c0, c1 in ((CS[0], 0, n), (CS[-1], n, NC)):
                    for k in range(KC):
                        link_w(dve.tensor_tensor(b1_v[0:rows, :, c0:c1], b1_v[0:rows, :, c0:c1],
                                                 banks[f"P{k}"][0:rows, 0:2 * NC].rearrange("p (g c) -> p g c", g=2)[:, :, c0:c1], ALU.add))
                link_w.wait()
                assert link_w.n == LINKS_W, link_w.n
                stand_alone(dve, waited_dve)
                with dve.Fori(0, TURNS) as tp:
                    u = l * TURNS + tp
                    link.turn, link.n = u, 0
                    for p in range(2):
                        base_n = u * 2 * B + B * p

                        def h_split(b):
                            dve.wait_ge(hhi_ready, base_n + b + 1)
                            ps = banks[slots.slot["h_t", B * p + b]]
                            dve.tensor_tensor(h_lo[:, b % 2].rearrange("p k n -> p (k n)"), ps[:, 0:D],
                                              h_hi[:, b % 2].rearrange("p k n -> p (k n)").bitcast(F32), ALU.subtract).then_inc(h_ready, 1)

                        def norms(b):
                            n = base_n + b
                            dve.wait_ge(sq_ready, n + 1)
                            dve.tensor_reduce(ss[:, :], t2[:, :, :], AX, ALU.add).then_inc(sq_used, 1)
                            dve.wait_ge(tab_ready, 2 * u + p + 1)
                            if B * p + b >= 1:
                                filled(dve, u, "k_t", B * p + b - 1)
                            for a in range(2):
                                ins = dve.tensor_tensor(t1[:, LH * a:LH * a + LH, :], qk[:, b % 2, LH * a:LH * a + LH, :],
                                                        tab[:, p, 2 * a, :].unsqueeze(1).to_broadcast([P, LH, HD]), ALU.mult)
                                if a == 0:
                                    link.done(ins)
                                else:
                                    ins.then_inc(t1_ready, 1)
                            dve.wait_ge(sq_used, n + 1)
                            link(dve.tensor_scalar(ss[:, :], ss[:, :], NORM_EPS ** 2, None, ALU.max))
                            rsqrt(dve, link, rn[:, b, :], ss[:, :], ra[:, :])
                            link(dve.tensor_scalar(rn[:, b, 0:LH], rn[:, b, 0:LH], QK_SCALE, None, ALU.mult))

                        def rotated(b):
                            n = base_n + b
                            dve.wait_ge(t1_ready, n + 1)
                            dve.wait_ge(t2_ready, 4 * n + 4)
                            link(dve.tensor_tensor(t1[:, LH:, :], t1[:, LH:, :], t2[:, LH:, :], ALU.add))
                            link(dve.tensor_tensor(t1[:, LH:, :], t1[:, LH:, :],
                                                   rn[:, b, LH:].unsqueeze(2).to_broadcast([P, LH, HD]), ALU.mult))
                            dve.tensor_tensor(t1[:, 0:LH, :], t1[:, 0:LH, :], t2[:, 0:LH, :], ALU.add).then_inc(rot_ready, 1)

                        def q_out(b):
                            ps = filled(dve, u, "q_t", B * p + b)
                            for e in range(2):
                                rows = slice(HD * e, HD * e + HD)
                                dve.tensor_copy(qt[rows, b % 2, e:LH:2, :], ps[rows, :].rearrange("p (c n) -> p c n", c=PAIRS)).then_inc(qt_ready, 1)

                        def maxima(r):
                            n = (2 * u + p) * B * PAIRS + r
                            ps = filled(dve, u, "s", B * PAIRS * p + r)
                            dve.wait_ge(mask_loaded, 16 * (u + 1))
                            if B * PAIRS * p + r >= 4:
                                filled(dve, u, "p_t", B * PAIRS * p + r - 4)
                            stand_alone(dve, waited_dve)
                            for e in range(2):
                                dve.tensor_tensor_reduce(sm[:, r % 4, e, :], ps[:, 2 * P * e:2 * P * e + 2 * P], mask[:, p, :], 1.0, -3.0e38,
                                                         ALU.add, ALU.max, mx[:, r % 4, e:e + 1]).then_inc(sm_ready, 1)
                            dve.wait_ge(sm_ready, 2 * n + 2)
                            h = 2 * (r % PAIRS)
                            dve.scalar_tensor_tensor(out=nb[:, r % 4, :], in0=mx[:, r % 4, :], scalar=-1.0,
                                                     in1=rn[:, r // PAIRS, h:h + 2], op0=ALU.mult, op1=ALU.mult).then_inc(nb_ready, 1)

                        def inverse(r):
                            n = (2 * u + p) * B * PAIRS + r
                            dve.wait_ge(ex_ready, 2 * n + 2)
                            dve.reciprocal(rinv[:, r % 4, :], rsum[:, r % 4, :]).then_inc(ri_ready, 1)

                        def o_split(b):
                            dve.wait_ge(ohi_ready, base_n + b + 1)
                            dve.tensor_tensor(o_lo[:, b % 2].rearrange("p c n -> p (c n)"), banks[f"O{b % 2}"][:, :],
                                              o_hi[:, b % 2].rearrange("p c n -> p (c n)").bitcast(F32), ALU.subtract).then_inc(o_ready, 1)

                        def residual(b):
                            ps = filled(dve, u, "wo", B * p + b)
                            dve.tensor_tensor(xs[:, p, b, 0:3:2, :], ps[:, 0:D].rearrange("p (c n) -> p c n", c=2),
                                              xs[:, p, b, 0:3:2, :], ALU.add).then_inc(x1_ready, 1)

                        def layer_norm(b):
                            dve.wait_ge(sh_loaded[b], 16 * (2 * u + p + 1))
                            dve.wait_ge(x1_ready, base_n + b + 1)
                            link(dve.bn_stats(st[:, :], xs[:, p, b, 0:2, :]))
                            stand_alone(dve, waited_dve)
                            link(dve.bn_aggr(mv[:, :], st[:, :]))
                            link(dve.tensor_scalar(var[:, :], mv[:, 1:2], LN_EPS, None, ALU.add))
                            rsqrt(dve, link, rs[:, :], var[:, :], tmp[:, :])
                            if B * p + b >= 2:
                                filled(dve, u, "x_t", B * p + b - 2)
                            dve.tensor_scalar(xn[:, b % 2, :].rearrange("p (c n) -> p c n", c=2), xs[:, p, b, 0:2, :], mv[:, 0:1], rs[:, 0:1],
                                              ALU.subtract, ALU.mult).then_inc(xn_ready[p], 1)
                            dve.wait_ge(xn_ready[p], B * u + b + 1)

                        def f_split(b):
                            dve.wait_ge(fhi_ready, base_n + b + 1)
                            ps = banks[slots.slot["x_t", B * p + b]]
                            dve.tensor_tensor(f_lo[:, :, P * b:P * b + P], ps[:, 0:D].rearrange("p (k n) -> p k n", k=KC),
                                              f_hi[:, :, P * b:P * b + P].bitcast(F32), ALU.subtract).then_inc(f_ready, 1)

                        h_split(0), h_split(1), norms(0), rotated(0), h_split(2), norms(1), q_out(0)
                        for r in range(B * PAIRS + 5):
                            b, j = divmod(r, PAIRS)
                            if b < B:
                                maxima(r)
                            if r >= 1 and r - 1 < B * PAIRS:
                                inverse(r - 1)
                            if b + 1 < B and j == 0:
                                rotated(b + 1)
                            if b + 1 < B and j == 2:
                                q_out(b + 1)
                            if b + 3 < B and j == 3:
                                h_split(b + 3)
                            if b + 2 < B and j == 3:
                                norms(b + 2)
                            if r >= 7 and j == 3:
                                o_split(b - 1)
                            if r >= 8 and j == 0:
                                residual(b - 2)
                            if r >= 12 and j == 1:
                                layer_norm(b - 3)
                        layer_norm(2)
                        f_split(0), f_split(1)
                        layer_norm(3)
                        f_split(2), f_split(3)
                        for j in range(NC):
                            m = (2 * u + p) * NC + j
                            ps = filled(dve, u, "a", NC * p + j)
                            dve.wait_ge(ge_ready, m + 1)
                            if NC * p + j >= 2:
                                dve.wait_ge(u_ready, m - 1)
                            dve.scalar_tensor_tensor(out=up[0:CS[j], j % 2, :], in0=ps[0:CS[j], :], scalar=b1[0:CS[j], j:j + 1],
                                                     in1=ge[0:CS[j], j % 2, :], op0=ALU.add, op1=ALU.mult).then_inc(up_ready, 1)
                        for b in range(B):
                            dve.wait_ge(w2_done, B * NC * (2 * u + p + 1))
                            dve.wait_ge(xb_ready[p], B * u + b + 1)
                            dve.tensor_tensor(yb[:, b, :], banks[f"O{b // 2}"][:, D * (b % 2):D * (b % 2) + D], yb[:, b, :],
                                              ALU.add).then_inc(y_ready, 1)
                        for b in range(B):
                            dve.wait_ge(gy_ready, base_n + b + 1)
                            dve.wait_ge(base_loaded[b], 16 * (2 * u + p + 1))
                            dve.scalar_tensor_tensor(out=yb[:, b, :], in0=base[:, b, :], scalar=flag[:, 0:1], in1=yb[:, b, :],
                                                     op0=ALU.mult, op1=ALU.add).then_inc(y2_ready, 1)
                    assert link.n == LINKS, link.n

        @block.tensor
        def _(pe):
            pe.wait_ge(preset, 3)
            with pe.Fori(0, NL) as l:
                pe.wait_ge(par_loaded, 16 * (6 + 2 + 2 * NC + 3) * (l + 1))
                for k in range(KC):
                    i = 3 + k
                    pe.wait_ge(w_loaded[i % 2], 16 * ([3, 4][i % 2] * l + [3, 2][i % 2]))
                    for g in range(2):
                        for j in range(NC):
                            c = HID * g + CO[j]
                            last = pe.matmul(banks[f"P{k}"][0:CS[j], NC * g + j:NC * g + j + 1], stage[i % 2][:, c:c + CS[j]],
                                             gb[:, 1, k:k + 1], start=True, stop=True)
                    last.then_inc(bias_done, 1)
                pe.wait_ge(w_lo, STAGED * (l + 1))
                pe.wait_ge(chain_w, LINKS_W * (l + 1))
                stand_alone(pe, waited_pe)
                with pe.Fori(0, TURNS) as tp:
                    u = l * TURNS + tp
                    for p in range(2):
                        base_n = u * 2 * B + B * p

                        def h_transpose(b):
                            ps = fill(pe, u, "h_t", B * p + b)
                            pe.wait_ge(xs_loaded[p][b], 32 * (u + 1))
                            for k in range(KC):
                                last = pe.transpose(ps[:, P * k:P * k + P], xs[:, p, b, k, :], ident[:, :])
                            last.then_inc(done["h_t"], 1)

                        def qkv(b):
                            parts = [(h_hi[:, b % 2, k, :], h_lo[:, b % 2, k, :]) for k in range(KC)]
                            for a in range(3):
                                kind, i = ("qk", 2 * (B * p + b) + a) if a < 2 else ("v", B * p + b)
                                ps = fill(pe, u, kind, i)
                                if a == 0:
                                    pe.wait_ge(h_ready, base_n + b + 1)
                                cols = slice(INNER * a, INNER * a + INNER)
                                split3(pe, ps[:, :], parts, [(wqkv[0][:, k, cols], wqkv[1][:, k, cols]) for k in range(KC)]).then_inc(done[kind], 1)

                        def qk_transpose(b):
                            for kind, c in (("q_t", 0), ("k_t", INNER)):
                                ps = fill(pe, u, kind, B * p + b)
                                pe.wait_ge(rot_ready, base_n + b + 1)
                                rows = t1[:, :, :].rearrange("p h d -> p (h d)")
                                for j in range(PAIRS):
                                    last = pe.transpose(ps[:, P * j:P * j + P], rows[:, c + P * j:c + P * j + P], ident[:, :])
                                last.then_inc(done[kind], 1)

                        def scores(r):
                            b, j = divmod(r, PAIRS)
                            ps = fill(pe, u, "s", B * PAIRS * p + r)
                            pe.wait_ge(qt_ready, 2 * (base_n + b) + 2)
                            pe.wait_ge(kt_ready, base_n + b + 1)
                            for e in range(2):
                                last = pe.matmul(ps[:, 2 * P * e:2 * P * e + 2 * P], qt[:, b % 2, 2 * j + e, :],
                                                 kt[:, b, j].rearrange("p w n -> p (w n)"), start=True, stop=True)
                            last.then_inc(done["s"], 1)

                        def values(r):
                            b, j = divmod(r, PAIRS)
                            n = (2 * u + p) * B * PAIRS + r
                            ps = fill(pe, u, "p_t", B * PAIRS * p + r)
                            pe.wait_ge(pn_ready, n + 1)
                            for e in range(2):
                                for w in range(2):
                                    c = P * (2 * e + w)
                                    last = pe.transpose(ps[:, c:c + P], sm[:, r % 4, e, P * w:P * w + P], ident[:, :])
                            last.then_inc(done["p_t"], 1)
                            if j == 0:
                                fill(pe, u, "o", B * p + b)
                            pe.wait_ge(v_ready, base_n + b + 1)
                            pe.wait_ge(pt_ready, n + 1)
                            for e in range(2):
                                c = HD * (2 * j + e)
                                for w in range(2):
                                    last = pe.matmul(banks[f"O{b % 2}"][HD * e:HD * e + HD, P * j:P * j + P], vt[:, b, w, c:c + HD],
                                                     pt[:, r % 2, 2 * e + w, :], start=(w == 0), stop=(w == 1))
                            last.then_inc(pv_done, 1)

                        def project(b):
                            ps = fill(pe, u, "wo", B * p + b)
                            pe.wait_ge(o_ready, base_n + b + 1)
                            split3(pe, ps[:, 0:D], [(o_hi[:, b % 2, c, :], o_lo[:, b % 2, c, :]) for c in range(PAIRS)],
                                   [(wo[0][:, c, :], wo[1][:, c, :]) for c in range(PAIRS)]).then_inc(done["wo"], 1)

                        h_transpose(0), h_transpose(1), qkv(0), qkv(1), h_transpose(2), qk_transpose(0)
                        for r in range(B * PAIRS + 5):
                            b, j = divmod(r, PAIRS)
                            if b < B:
                                scores(r)
                            if b + 2 < B and j == 0:
                                qkv(b + 2)
                            if 0 <= r - LAG < B * PAIRS:
                                values(r - LAG)
                            if b + 1 < B and j == 2:
                                qk_transpose(b + 1)
                            if b + 3 < B and j == 3:
                                h_transpose(b + 3)
                            if r >= 8 and j == 0:
                                project(b - 2)
                        for b in range(B):
                            ps = fill(pe, u, "x_t", B * p + b)
                            pe.wait_ge(xn_ready[p], B * u + b + 1)
                            for k in range(KC):
                                last = pe.transpose(ps[:, P * k:P * k + P], xn[:, b % 2, P * k:P * k + P], ident[:, :])
                            last.then_inc(done["x_t"], 1)
                        pe.wait_ge(f_ready, base_n + B)

                        def hidden(kind, j):
                            ps = fill(pe, u, kind, NC * p + j)
                            c = CO[j] + (HID if kind == "g" else 0)
                            split3(pe, ps[0:CS[j], :], [(w1[0][:, k, c:c + CS[j]], w1[1][:, k, c:c + CS[j]]) for k in range(KC)],
                                   [(f_hi[:, k, :], f_lo[:, k, :]) for k in range(KC)]).then_inc(done[kind], 1)

                        for j in range(NC + 1):
                            if j < NC:
                                hidden("a", j)
                                hidden("g", j)
                            if j == 1:
                                fill(pe, u, "y", 2 * p)
                                fill(pe, u, "y", 2 * p + 1)
                            if j >= 1:
                                k = j - 1
                                pe.wait_ge(u_ready, (2 * u + p) * NC + k + 1)
                                n = CS[k]
                                for b in range(B):
                                    ps = banks[f"O{b // 2}"][:, D * (b % 2):D * (b % 2) + D]
                                    cols = slice(P * b, P * b + P)
                                    pe.matmul(ps, u_hi[0:n, k % 2, cols], w2[0][0:n, k, :], start=(k == 0 and b % 2 == 0), stop=False, skip_group_check=True)
                                    pe.matmul(ps, u_hi[0:n, k % 2, cols], w2[1][0:n, k, :], start=False, stop=False, skip_group_check=True)
                                    pe.matmul(ps, u_lo[0:n, k % 2, cols], w2[0][0:n, k, :], start=False, stop=(k == NC - 1), skip_group_check=True).then_inc(w2_done, 1)


def constants():
    f32 = np.float32
    half = np.arange(0, HD, 2, dtype=f32)
    pos = np.arange(N, dtype=f32)
    freqs = pos[:, None] * (f32(1.0) / f32(10000.0) ** (half / f32(HD)))
    xbase = (half + f32(0.4 * HD)) / f32(1.4 * HD)
    scale = xbase[None, :] ** ((pos[:, None] - N // 2) / f32(P // 2))
    cos, sin = np.cos(freqs), np.sin(freqs)
    tabs = [np.concatenate(t, axis=-1) for f in (scale, 1.0 / scale)
            for t in ((cos * f, cos * f), (-sin * f, sin * f))]
    rope = np.stack(tabs, axis=1).reshape(NT, P, 4, HD)
    q, k = np.arange(P)[:, None], np.arange(P)[None, :]
    own = np.where(k <= q, 0.0, BIG)
    before = np.where(k >= q, 0.0, BIG)
    mask = np.zeros((TURNS, P, 2, 2 * P))
    mask[:, :, 0] = np.concatenate([own, before], axis=1)
    mask[:, :, 1] = np.concatenate([before, own], axis=1)
    mask[0, :, 0, P:] = BIG
    flags = np.array([[float(l == NL - 1)] for l in range(NL)])
    return {k: v.astype(np.float32) for k, v in
            {"ident": np.eye(P), "rope": rope, "mask": mask, "flags": flags}.items()}


def build(nc, io, out, kind="Internal"):
    def dram(name, shape):
        return nc.dram_tensor(name, shape, F32, kind=kind).ap() if kind != "Internal" else nc.dram_tensor(name, shape, F32).ap()

    scratch = {
        "mod": dram("mod_rows", (B, 6 * D)),
        "gate": dram("gate_rows", (2, B, D)),
        "x": dram("x_layers", (3, B, N + 1, D)),
        "xa": dram("x_attended", (B, N + 1, D)),
        "base": dram("base_rows", (B, N, D)),
    }
    with ExitStack() as ctx:
        def sb(name, shape, dt=F32):
            return ctx.enter_context(nc.sbuf_tensor(name, shape, dt))

        ident = sb("ident", [P, P])
        with ExitStack() as inner:
            def sb1(name, shape, dt=F32):
                return inner.enter_context(nc.sbuf_tensor(name, shape, dt))

            w = {"ident": ident, "hi": sb1("wt_hi", [P, KC, 4 * D], F32R), "lo": sb1("wt_lo", [P, KC, 4 * D], F32R),
                 "gamma": sb1("gamma", [P, 2, HD]), "bo": sb1("bo", [P, D]), "ln": sb1("ln_cols", [P, 2, KC])}
            setup_block(nc, io, scratch, w)
            attention_block(nc, io, scratch, w)
        layers_block(nc, io, scratch, out, ident)


_INS = {"x": "L0_attn_x", "ln_gamma": "L0_attn_ln_gamma", "ln_beta": "L0_attn_ln_beta", "q_gamma": "L0_attn_q_gamma",
        "k_gamma": "L0_attn_k_gamma", "wq": "L0_attn_w_q", "wk": "L0_attn_w_k", "wv": "L0_attn_w_v",
        "wo": "L0_attn_w_o", "bo": "L0_attn_b_o", "wqkv": "L0_ffn_wqkv", "q_scale": "L0_ffn_q_scale",
        "k_scale": "L0_ffn_k_scale", "f_wo": "L0_ffn_wo", "lg": "L0_ffn_ln_g", "lb": "L0_ffn_ln_b",
        "w1": "L0_ffn_w1", "b1": "L0_ffn_b1", "w2": "L0_ffn_w2", "b2": "L0_ffn_b2", "c": "L0_c", "wmod": "L0_wmod"}


def kernel(**inputs):
    import concourse.bacc as bacc
    from concourse.bass_utils import run_bass_kernel_spmd

    nc = bacc.Bacc("TRN2", target_bir_lowering=False, num_devices=1)
    arrays = {f"in_{k}": np.ascontiguousarray(inputs[name]) for k, name in _INS.items()}
    arrays.update({f"in_{k}": v for k, v in constants().items()})
    io = {k[3:]: nc.dram_tensor(k, a.shape, mybir.dt.from_np(a.dtype), kind="ExternalInput").ap() for k, a in arrays.items()}
    out = nc.dram_tensor("out_0", (B, N, D), F32, kind="ExternalOutput").ap()
    build(nc, io, out)
    result = run_bass_kernel_spmd(nc, [arrays], core_ids=[0])
    return result.results[0]["out_0"]
```

```python
from contextlib import ExitStack

import numpy as np

import concourse.bass as bass
from concourse import mybir

F32 = mybir.dt.float32
F32R = mybir.dt.float32r
U32 = mybir.dt.uint32
I32 = mybir.dt.int32
ALU = mybir.AluOpType
ACT = mybir.ActivationFunctionType
AX = mybir.AxisListType.X

P = 128
B, N, D = 4, 1024, 256
NT = N // P
KC = D // P
GH, HD = 4, 64
HALF = N // 2
LN_EPS = 1e-5
RMS_EPS = 1e-8
MAGIC = 0x5F3759DF
RSQRT_LINKS = 11


class Slots:

    TURNS = 3

    def __init__(self, body, tensors, done, release, ahead=()):
        self.tensors, self.done, self.release = tensors, done, release
        self.phase = "body"
        ahead = set(ahead)
        self.slot = {(k, i): s for k, i, s in body}
        self.per_turn = {}
        for k, i in self.slot:
            self.per_turn[k] = max(self.per_turn.get(k, 0), i + 1)
        uses = []
        for first in (0, self.TURNS):
            uses += [(first, "first", k, i) for k, i, _ in body if (k, i) in ahead]
            for turn in range(first, first + self.TURNS):
                last = turn == first + self.TURNS - 1
                uses += [(turn + ((k, i) in ahead), "last" if last else "body", k, i)
                         for k, i, _ in body if not (last and (k, i) in ahead)]
        self.before, holder, seen = {}, {}, {}
        for turn, phase, k, i in uses:
            assert i == seen.get(k, 0) % self.per_turn[k], (k, i)
            seen[k] = seen.get(k, 0) + 1
            before = holder.get(self.slot[k, i])
            holder[self.slot[k, i]] = (turn, k, i)
            if before is None:
                continue
            t, kb, ib = before
            if t < turn and ((k, i) not in ahead or phase == "first"):
                assert seen[kb] >= turn * self.per_turn[kb], (k, i, before)
                ib = self.per_turn[kb] - 1
            here = (kb, t - turn, ib)
            self.before.setdefault((phase, k, i), set()).add(here)
        for phase in ("first", "body", "last"):
            for k, i in self.slot:
                assert (phase, k, i) in self.before or (k, i) in ahead or phase == "first", (phase, k, i)

    def fill(self, eng, turn, kind, i):
        for k, t, j in sorted(self.before[self.phase, kind, i]):
            for sem, n in self.release[k]:
                eng.wait_ge(sem, (turn * self.per_turn[k] + (t * self.per_turn[k] + j + 1)) * n)
        return self.tensors[self.slot[kind, i]]

    def filled(self, eng, turn, kind, i):
        eng.wait_ge(self.done[kind], turn * self.per_turn[kind] + i + 1)
        return self.tensors[self.slot[kind, i]]


def stand_alone(eng, waited):
    eng.sem_inc(waited, 1)


class Link:

    def __init__(self, eng, sem, per_turn=0):
        self.eng, self.sem, self.per_turn, self.turn, self.n = eng, sem, per_turn, 0, 0

    def __call__(self, ins):
        self.n += 1
        ins.then_inc(self.sem, 1)
        self.eng.wait_ge(self.sem, self.turn * self.per_turn + self.n)

    def done(self, ins):
        self.n += 1
        ins.then_inc(self.sem, 1)

    def wait(self):
        self.eng.wait_ge(self.sem, self.turn * self.per_turn + self.n)


def rsqrt(dve, link, y, v, a):
    link(dve.tensor_scalar(a.bitcast(U32), v.bitcast(U32), 1, None, ALU.logical_shift_right))
    link(dve.tensor_scalar(y.bitcast(I32), a.bitcast(I32), -1.0, float(MAGIC), ALU.mult, ALU.add))
    for _ in range(3):
        link(dve.scalar_tensor_tensor(out=a, in0=y, scalar=-0.5, in1=y, op0=ALU.mult, op1=ALU.mult))
        link(dve.tensor_tensor(a, a, v, ALU.mult))
        link(dve.scalar_tensor_tensor(out=y, in0=a, scalar=1.5, in1=y, op0=ALU.add, op1=ALU.mult))


def setup_block(nc, io, scratch, w):
    with ExitStack() as ctx:
        def sb(name, shape, dt=F32):
            return ctx.enter_context(nc.sbuf_tensor(name, shape, dt))

        def sem(name):
            return ctx.enter_context(nc.semaphore(name))

        c_t = sb("c_t", [P, KC, B])
        c_exp = sb("c_exp", [P, KC, B])
        c_silu = sb("c_silu", [P, KC, B])
        wmod = sb("wmod", [P, KC, 6 * D])
        raw = sb("raw", [P, 4, KC, D])
        mod = sb("mod", [B, 6 * D])
        sign = sb("sign", [B, D])
        mag = sb("mag", [B, D])
        ones = sb("ones", [B, D])
        zeros = sb("zeros", [B, D])
        mod_ps = ctx.enter_context(nc.psum_tensor("mod_ps", [P, 3, 512], F32))
        wt_ps = ctx.enter_context(nc.psum_tensor("wt_ps", [P, KC, 2, 512], F32))

        loaded = sem("loaded")
        loaded_w = sem("loaded_w")
        const_set = sem("const_set")
        exp_done = sem("exp_done")
        silu_done = sem("silu_done")
        mod_done = sem("mod_done")
        wt_done = sem("wt_done")
        hi_done = sem("hi_done")
        mod_ready = sem("mod_ready")
        stored = sem("stored")
        chain = sem("setup_chain")
        block = ctx.enter_context(nc.Block())

        @block.sync
        def _(sp):
            with nc.allow_non_contiguous_dma(reason="1024 words of c, transposed"):
                for k in range(KC):
                    sp.dma_start(c_t[:, k, :], io["c"].rearrange("b (k p) -> k p b", k=KC)[k]).then_inc(loaded, 16)
            sp.dma_start(wmod[:, :, :], io["wmod"].rearrange("(k p) n -> p k n", k=KC)).then_inc(loaded, 16)
            for i, name in enumerate(("wq", "wk", "wv", "wo")):
                sp.dma_start(raw[:, i, :, :], io[name].rearrange("(o p) n -> p o n", o=KC)).then_inc(loaded_w, 16)
            sp.dma_start(w["ident"][:, :], io["ident"]).then_inc(loaded_w, 16)
            for i, name in enumerate(("q_gamma", "k_gamma")):
                sp.dma_start(w["gamma"][:, i, :], io[name].unsqueeze(0).to_broadcast([P, HD])).then_inc(loaded_w, 16)
            sp.dma_start(w["bo"][:, :], io["bo"].unsqueeze(0).to_broadcast([P, D])).then_inc(loaded_w, 16)
            with nc.allow_non_contiguous_dma(reason="feature columns of the layer norm's gain and bias"):
                for i, name in enumerate(("ln_gamma", "ln_beta")):
                    sp.dma_start(w["ln"][:, i, :], io[name].rearrange("(k p) -> p k", k=KC)).then_inc(loaded_w, 16)
            sp.wait_ge(const_set, 2)
            for l in range(2):
                sp.dma_start(scratch["x"][l, :, 0, :], zeros[:, :]).then_inc(stored, 16)
            sp.dma_start(scratch["xa"][:, 0, :], zeros[:, :]).then_inc(stored, 16)
            sp.dma_start(scratch["gate"][0], ones[:, :]).then_inc(stored, 16)
            sp.wait_ge(mod_ready, 1)
            sp.dma_start(scratch["mod"], mod[:, :]).then_inc(stored, 16)
            sp.dma_start(scratch["gate"][1], mod[:, 5 * D:6 * D]).then_inc(stored, 16)
            sp.wait_ge(stored, 6 * 16)
            sp.wait_ge(loaded_w, 10 * 16)

        @block.scalar
        def _(act):
            act.wait_ge(loaded, 48)
            act.activation(c_exp[:, :, :], c_t[:, :, :], ACT.Exp, scale=-1.0).then_inc(exp_done, 1)
            for k in range(KC):
                for j in range(2):
                    act.wait_ge(wt_done, 2 * k + j + 1)
                    act.copy(w["hi"][:, k, 512 * j:512 * j + 512], wt_ps[:, k, j, :]).then_inc(hi_done, 1)

        @block.tensor
        def _(pe):
            pe.wait_ge(silu_done, 1)
            for n in range(3):
                for k in range(KC):
                    last = pe.matmul(mod_ps[0:B, n, :], c_silu[:, k, :], wmod[:, k, 512 * n:512 * n + 512],
                                     start=(k == 0), stop=(k == KC - 1))
            last.then_inc(mod_done, 1)
            pe.wait_ge(loaded_w, 10 * 16)
            for k in range(KC):
                for j in range(2):
                    for i in range(2):
                        for o in range(KC):
                            last = pe.transpose(wt_ps[:, k, j, D * i + P * o:D * i + P * o + P],
                                                raw[:, 2 * j + i, o, P * k:P * k + P], w["ident"][:, :])
                    last.then_inc(wt_done, 1)

        @block.vector
        def _(dve):
            link = Link(dve, chain)
            dve.memset(zeros[:, :], 0.0).then_inc(const_set, 1)
            dve.memset(ones[:, :], 1.0).then_inc(const_set, 1)
            dve.wait_ge(loaded, 48)
            dve.wait_ge(exp_done, 1)
            link(dve.tensor_scalar(c_exp[:, :, :], c_exp[:, :, :], 1.0, None, ALU.add))
            link(dve.reciprocal(c_exp[:, :, :], c_exp[:, :, :]))
            dve.tensor_tensor(c_silu[:, :, :], c_t[:, :, :], c_exp[:, :, :], ALU.mult).then_inc(silu_done, 1)
            dve.wait_ge(mod_done, 1)
            link(dve.tensor_copy(mod[:, :].rearrange("b (n m) -> b n m", n=3), mod_ps[0:B, :, :]))
            for i in (1, 4):
                link(dve.tensor_scalar(mod[:, D * i:D * i + D], mod[:, D * i:D * i + D], 1.0, None, ALU.add))
            for i in (2, 5):
                g = mod[:, D * i:D * i + D]
                link(dve.tensor_scalar(sign[:, :], g, 0.0, 2.0, ALU.is_ge, ALU.mult))
                link(dve.tensor_scalar(mag[:, :], g, -1.0, None, ALU.mult))
                link(dve.tensor_tensor(mag[:, :], mag[:, :], g, ALU.max))
                link(dve.tensor_scalar(mag[:, :], mag[:, :], 0.25, None, ALU.max))
                last = dve.scalar_tensor_tensor(out=g, in0=sign[:, :], scalar=-1.0, in1=mag[:, :],
                                                op0=ALU.add, op1=ALU.mult)
                if i == 2:
                    link(last)
            last.then_inc(mod_ready, 1)
            for i in range(2 * KC):
                dve.wait_ge(hi_done, i + 1)
                k, j = i // 2, i % 2
                dve.tensor_tensor(w["lo"][:, k, 512 * j:512 * j + 512], wt_ps[:, k, j, :],
                                  w["hi"][:, k, 512 * j:512 * j + 512].bitcast(F32), ALU.subtract)
            dve.wait_ge(loaded_w, 10 * 16)
            link(dve.tensor_scalar(w["gamma"][:, 0, :], w["gamma"][:, 0, :], float(HD) ** -0.5, None, ALU.mult))


def split3(pe, out, parts, wide, start=True, stop=True):
    last = None
    n = len(parts)
    for k, ((a_hi, a_lo), (b_hi, b_lo)) in enumerate(zip(parts, wide)):
        pe.matmul(out, a_hi, b_hi, start=(start and k == 0), stop=False)
        pe.matmul(out, a_hi, b_lo, start=False, stop=False)
        last = pe.matmul(out, a_lo, b_hi, start=False, stop=(stop and k == n - 1))
    return last


def attention_block(nc, io, scratch, w):
    with ExitStack() as ctx:
        def sb(name, shape, dt=F32):
            return ctx.enter_context(nc.sbuf_tensor(name, shape, dt))

        def sem(name):
            return ctx.enter_context(nc.semaphore(name))

        tensors = {s: ctx.enter_context(nc.psum_tensor(f"ps_{s}", [P, 2, 512], F32)) for s in ("A0", "A1", "M", "O")}
        order = []
        for i in range(NT + 1):
            if i < NT:
                order.append(("x_t", i, ("M", "O")[i % 2]))
            if i >= 1:
                order.append(("qkv", i - 1, ("A0", "A1")[(i - 1) % 2]))
        for i in range(NT):
            order.append(("qk_t", i, ("A0", "A1")[i % 2]))
            order.append(("kl_t", i, ("M", "O")[i % 2]))
        for i in range(NT):
            order.append(("max", i, ("M", "A0", "A1")[i % 3]))
        order.append(("m_t", 0, "M"))
        for h in range(GH):
            order.append(("out", h, "O"))
            for i in range(NT):
                order.append(("s_t", NT * h + i, ("A0", "A1")[i % 2]))
                if h + 1 < GH:
                    order.append(("max", NT * (h + 1) + i, "M"))
            if h + 1 < GH:
                order.append(("m_t", h + 1, "M"))
            order.append(("back", h, "M"))
        for i in range(NT):
            order.append(("y_t", i, ("M", "O")[i % 2]))
            order.append(("wo", i, ("A0", "A1")[i % 2]))

        x8 = sb("x8", [P, NT, D])
        h8 = sb("h8", [P, NT, D])
        mrow = sb("mrow", [P, 6, D])
        st = sb("st", [P, NT, 6])
        mv = sb("mv", [P, NT, 2])
        rs = sb("rs", [P, NT])
        var = sb("var", [P, NT])
        tmp = sb("tmp", [P, NT])
        x_f = sb("x_f", [P, 2, KC, P])
        x_hi = sb("x_hi", [P, 2, KC, P], F32R)
        x_lo = sb("x_lo", [P, 2, KC, P], F32R)
        qk8 = sb("qk8", [P, NT, 2 * GH * HD])
        sq = sb("sq", [P, 2, 2 * GH * HD])
        ss = sb("ss", [P, NT * 2 * GH])
        rr = sb("rr", [P, NT * 2 * GH])
        rt = sb("rt", [P, NT * 2 * GH])
        qn = sb("qn", [P, 2, 2, GH, HD])
        q_s = sb("q_s", [P, NT, GH, 3 * HD], F32R)
        k_s = sb("k_s", [P, 2, GH, 4 * HD], F32R)
        q1 = sb("q1", [P, GH, N], F32R)
        k1 = sb("k1", [P, GH, N], F32R)
        k2 = sb("k2", [P, GH, N], F32R)
        q2 = sb("q2", [P, 2, N], F32R)
        v1 = sb("v1", [P, NT, GH, HD + 1])
        pr = sb("pr", [P, 3, N])
        mx = sb("mx", [P, 2, NT])
        o_t = sb("o_t", [HD + 1, N])
        rc = sb("rc", [P, 2, 4])
        y_hi = sb("y_hi", [P, 2, KC, P], F32R)
        y_lo = sb("y_lo", [P, 2, KC, P], F32R)
        yb = sb("yb", [P, 2, D])
        one = sb("one", [P, GH * HD])

        kinds = ("x_t", "qkv", "qk_t", "kl_t", "max", "m_t", "s_t", "back", "y_t", "wo")
        done = {k: sem(f"{k}_done") for k in kinds}
        x_loaded = sem("x_loaded")
        preset = sem("preset")
        waited_sp = sem("waited_sp")
        waited_dve = sem("waited_dve")
        xn_ready = sem("xn_ready")
        xf_ready = sem("xf_ready")
        xt_ready = sem("xt_ready")
        qk_ready = sem("qk_ready")
        v_ready = sem("v_ready")
        sq_ready = sem("sq_ready")
        sq_used = sem("sq_used")
        qn_ready = sem("qn_ready")
        qg_ready = sem("qg_ready")
        hi_ready = sem("hi_ready")
        s_ready = sem("s_ready")
        q1_ready = sem("q1_ready")
        k1_ready = sem("k1_ready")
        k2_ready = sem("k2_ready")
        max_ready = sem("max_ready")
        m_ready = sem("m_ready")
        q2_ready = sem("q2_ready")
        p_ready = sem("p_ready")
        p_used = sem("p_used")
        ot_ready = sem("ot_ready")
        o8_ready = sem("o8_ready")
        yhi_ready = sem("yhi_ready")
        y_ready = sem("y_ready")
        yb_ready = sem("yb_ready")
        yg_ready = sem("yg_ready")
        x2_ready = sem("x2_ready")
        h0_ready = sem("h0_ready")
        st_x2 = sem("st_x2")
        st_h0 = sem("st_h0")
        chain = sem("chain")
        done["out"] = p_used
        slots = Slots(order, tensors, done, {
            "x_t": [(xf_ready, KC)], "qkv": [(v_ready, 1)], "qk_t": [(q1_ready, 1), (k1_ready, 1)],
            "kl_t": [(k2_ready, 1)], "max": [(max_ready, 1)], "m_t": [(q2_ready, 1)], "s_t": [(p_ready, 1)],
            "out": [(ot_ready, 1)], "back": [(o8_ready, 2)], "y_t": [(y_ready, 1)], "wo": [(yb_ready, 1)]})
        fill, filled = slots.fill, slots.filled
        block = ctx.enter_context(nc.Block())

        @block.sync
        def _(sp):
            with sp.Fori(0, B) as it:
                sp.dma_start(x8[:, :, :], io["x"][bass.ds(it, 1)].rearrange("a (t p) d -> p (a t) d", p=P)).then_inc(x_loaded, 16)
                sp.dma_start(mrow[:, :, :].rearrange("p s d -> p (s d)"),
                             scratch["mod"][bass.ds(it, 1), :].to_broadcast([P, 6 * D])).then_inc(x_loaded, 16)
                sp.wait_ge(x2_ready, NT * (it + 1))
                sp.dma_start(scratch["base"][bass.ds(it, 1)].rearrange("a (t p) d -> p (a t) d", p=P), x8[:, :, :]).then_inc(st_x2, 16)
                sp.wait_ge(h0_ready, it + 1)
                sp.dma_start(scratch["x"][0, bass.ds(it, 1), 1:N + 1, :].rearrange("a (t p) d -> p (a t) d", p=P), h8[:, :, :]).then_inc(st_h0, 16)
                sp.wait_ge(st_x2, 16 * (it + 1))
                sp.wait_ge(st_h0, 16 * (it + 1))
                stand_alone(sp, waited_sp)

        @block.gpsimd
        def _(pool):
            pool.memset(one[:, :], 0.0).then_inc(preset, 1)
            pool.memset(v1[:, :, :, HD:HD + 1], 1.0).then_inc(preset, 1)
            with pool.Fori(0, B) as it:
                for i in range(NT):
                    pool.wait_ge(qn_ready, it * NT + i + 1)
                    pool.tensor_tensor(qn[:, i % 2], qn[:, i % 2],
                                       w["gamma"][:, :, :].unsqueeze(2).to_broadcast([P, 2, GH, HD]),
                                       ALU.mult).then_inc(qg_ready, 1)
                for i in range(NT):
                    pool.wait_ge(yb_ready, it * NT + i + 1)
                    pool.tensor_tensor(yb[:, i % 2, :], yb[:, i % 2, :], mrow[:, 2, :], ALU.mult).then_inc(yg_ready, 1)
                    pool.wait_ge(yg_ready, it * NT + i + 1)
                    pool.tensor_tensor(x8[:, i, :], x8[:, i, :], yb[:, i % 2, :], ALU.add).then_inc(x2_ready, 1)

        def qkv_out(act, it, i):
            ps = filled(act, it, "qkv", i)
            act.copy(qk8[:, i, :], ps[:, 0, :]).then_inc(qk_ready, 1)
            act.copy(v1[:, i, :, 0:HD], ps[:, 1, 0:GH * HD].rearrange("p (h d) -> p h d", h=GH)).then_inc(v_ready, 1)
            act.wait_ge(qk_ready, it * NT + i + 1)
            if i >= 2:
                act.wait_ge(sq_used, it * NT + i - 1)
            act.activation(sq[:, i % 2, :], qk8[:, i, :], ACT.Square).then_inc(sq_ready, 1)

        def q1_out(act, it, i):
            ps = filled(act, it, "qk_t", i)
            act.copy(q1[:, :, P * i:P * i + P], ps[:, 0, :].rearrange("p (h n) -> p h n", h=GH)).then_inc(q1_ready, 1)

        @block.scalar
        def _(act):
            act.wait_ge(preset, 2)
            with act.Fori(0, B) as it:
                for i in range(NT):
                    ps = filled(act, it, "x_t", i)
                    if i >= 2:
                        act.wait_ge(xt_ready, it * NT + i - 1)
                    for k in range(KC):
                        act.activation(x_f[:, i % 2, k, :], ps[:, 0, P * k:P * k + P], ACT.Identity,
                                       scale=w["ln"][:, 0, k:k + 1], bias=w["ln"][:, 1, k:k + 1]).then_inc(xf_ready, 1)
                    if i >= 1:
                        qkv_out(act, it, i - 1)
                qkv_out(act, it, NT - 1)
                for i in range(NT):
                    act.wait_ge(qg_ready, it * NT + i + 1)
                    if i >= 2:
                        filled(act, it, "kl_t", i - 2)
                    act.copy(q_s[:, i, :, HD:2 * HD], qn[:, i % 2, 0, :, :]).then_inc(hi_ready, 1)
                    act.copy(k_s[:, i % 2, :, 0:2 * HD].rearrange("p h (r d) -> p h r d", r=2),
                             qn[:, i % 2, 1, :, :].unsqueeze(2).to_broadcast([P, GH, 2, HD])).then_inc(hi_ready, 1)
                    if i >= 1:
                        q1_out(act, it, i - 1)
                q1_out(act, it, NT - 1)
                for h in range(GH):
                    for i in range(NT):
                        n = h * NT + i
                        ps = filled(act, it, "s_t", n)
                        if n >= 3:
                            act.wait_ge(p_used, it * GH * NT + n - 2)
                        act.activation(pr[:, n % 3, :].rearrange("p (a b) -> p a b", a=2), ps[:, :, :],
                                       ACT.Exp).then_inc(p_ready, 1)
                for i in range(NT):
                    ps = filled(act, it, "y_t", i)
                    if i >= 2:
                        filled(act, it, "wo", i - 2)
                    act.copy(y_hi[:, i % 2, :, :].rearrange("p k n -> p (k n)"), ps[:, 0, 0:D]).then_inc(yhi_ready, 1)

        LINKS = (3 * (2 * NT + 1 + RSQRT_LINKS) + 2 * NT) + 3 + NT + (1 + RSQRT_LINKS) + GH

        @block.vector
        def _(dve):
            link = Link(dve, chain, LINKS)
            dve.wait_ge(preset, 1)
            for i in range(NT):
                link.done(dve.tensor_copy(q_s[:, i, :, 2 * HD:3 * HD], one[:, :].rearrange("p (h d) -> p h d", h=GH)))
            for i in range(2):
                link.done(dve.tensor_copy(k_s[:, i, :, 3 * HD:4 * HD], one[:, :].rearrange("p (h d) -> p h d", h=GH)))
            link.wait()
            link(dve.memset(one[:, 0:1], 1.0))
            for i in range(2):
                link.done(dve.tensor_copy(k_s[:, i, :, 3 * HD:3 * HD + 1], one[:, 0:1].unsqueeze(1).to_broadcast([P, GH, 1])))
            link.wait()
            base = link.n

            def row(r):
                return mrow[:, r, :].unsqueeze(1).to_broadcast([P, NT, D])

            def layer_norm(src, dst, last=None):
                for i in range(NT):
                    link.done(dve.bn_stats(st[:, i, :], src[:, i, :]))
                link.wait()
                stand_alone(dve, waited_dve)
                for i in range(NT):
                    link.done(dve.bn_aggr(mv[:, i, :], st[:, i, :]))
                link.wait()
                link(dve.tensor_scalar(var[:, :], mv[:, :, 1], LN_EPS, None, ALU.add))
                rsqrt(dve, link, rs[:, :], var[:, :], tmp[:, :])
                for i in range(NT):
                    ins = dve.tensor_scalar(dst[:, i, :], src[:, i, :], mv[:, i, 0:1], rs[:, i:i + 1],
                                            ALU.subtract, ALU.mult)
                    if last is None:
                        link.done(ins)
                    else:
                        ins.then_inc(last, 1)
                if last is None:
                    link.wait()

            with dve.Fori(0, B) as it:
                link.turn, link.n = it, base
                dve.wait_ge(x_loaded, 32 * (it + 1))
                layer_norm(x8, h8)
                link(dve.tensor_tensor(h8[:, :, :], h8[:, :, :], row(1), ALU.mult))
                link(dve.tensor_tensor(h8[:, :, :], h8[:, :, :], row(0), ALU.add))
                layer_norm(h8, h8, last=xn_ready)

                def square_sum(i):
                    dve.wait_ge(sq_ready, it * NT + i + 1)
                    dve.tensor_reduce(ss[:, 2 * GH * i:2 * GH * (i + 1)],
                                      sq[:, i % 2, :].rearrange("p (g d) -> p g d", d=HD), AX, ALU.add).then_inc(sq_used, 1)

                for i in range(NT):
                    dve.wait_ge(xf_ready, 2 * (it * NT + i) + 2)
                    if i >= 2:
                        filled(dve, it, "qkv", i - 2)
                    link(dve.tensor_copy(x_hi[:, i % 2], x_f[:, i % 2]))
                    dve.tensor_tensor(x_lo[:, i % 2], x_f[:, i % 2], x_hi[:, i % 2].bitcast(F32),
                                      ALU.subtract).then_inc(xt_ready, 1)
                    if i >= 1:
                        square_sum(i - 1)
                square_sum(NT - 1)
                dve.wait_ge(sq_used, (it + 1) * NT)
                link(dve.tensor_scalar(ss[:, :], ss[:, :], 1.0 / HD, RMS_EPS ** 2, ALU.mult, ALU.max))
                rsqrt(dve, link, rr[:, :], ss[:, :], rt[:, :])

                def k_out(i):
                    ps = filled(dve, it, "qk_t", i)
                    dve.tensor_copy(k1[:, :, P * i:P * i + P], ps[:, 1, :].rearrange("p (h n) -> p h n", h=GH)).then_inc(k1_ready, 1)
                    ps = filled(dve, it, "kl_t", i)
                    dve.tensor_copy(k2[:, :, P * i:P * i + P], ps[:, 0, :].rearrange("p (h n) -> p h n", h=GH)).then_inc(k2_ready, 1)

                for i in range(NT):
                    if i >= 2:
                        dve.wait_ge(s_ready, 2 * (it * NT + i - 1))
                    dve.tensor_tensor(qn[:, i % 2].rearrange("p a h d -> p (a h) d"),
                                      qk8[:, i, :].rearrange("p (g d) -> p g d", d=HD),
                                      rr[:, 2 * GH * i:2 * GH * (i + 1)].unsqueeze(2).to_broadcast([P, 2 * GH, HD]),
                                      ALU.mult).then_inc(qn_ready, 1)
                    dve.wait_ge(hi_ready, 2 * (it * NT + i) + 2)
                    dve.tensor_tensor(q_s[:, i, :, 0:HD], qn[:, i % 2, 0], q_s[:, i, :, HD:2 * HD].bitcast(F32),
                                      ALU.subtract).then_inc(s_ready, 1)
                    dve.tensor_tensor(k_s[:, i % 2, :, 2 * HD:3 * HD], qn[:, i % 2, 1],
                                      k_s[:, i % 2, :, 0:HD].bitcast(F32), ALU.subtract).then_inc(s_ready, 1)
                    if i >= 1:
                        k_out(i - 1)
                k_out(NT - 1)

                def row_max(h, i):
                    ps = filled(dve, it, "max", NT * h + i)
                    dve.tensor_reduce(mx[:, h % 2, i:i + 1], ps[:, :, :].rearrange("p a b -> p (a b)"), AX, ALU.max).then_inc(max_ready, 1)

                def minus_max(h):
                    dve.wait_ge(max_ready, (it * GH + h + 1) * NT)
                    dve.tensor_scalar(q_s[:, :, h, 2 * HD:2 * HD + 1], mx[:, h % 2, :].unsqueeze(2), -1.0, None,
                                      ALU.mult).then_inc(m_ready, 1)
                    ps = filled(dve, it, "m_t", h)
                    if h >= 2:
                        filled(dve, it, "s_t", NT * (h - 1) - 1)
                    dve.tensor_copy(q2[:, h % 2, :].rearrange("p (a b) -> p a b", a=2), ps[:, :, :]).then_inc(q2_ready, 1)

                for i in range(NT):
                    row_max(0, i)
                minus_max(0)
                for h in range(GH):
                    if h + 1 < GH:
                        for i in range(NT):
                            row_max(h + 1, i)
                        minus_max(h + 1)
                    dve.wait_ge(p_used, (it * GH + h + 1) * NT)
                    ps = slots.tensors["O"]
                    dve.tensor_copy(o_t[:, :].rearrange("p (a b) -> p a b", a=2), ps[0:HD + 1, :, :]).then_inc(ot_ready, 1)
                    ps = filled(dve, it, "back", h)
                    back = ps[:, :, :].rearrange("p a (i n) -> p a i n", n=P)
                    link(dve.reciprocal(rc[:, :, :], back[:, :, :, HD]))
                    for a in range(2):
                        dve.tensor_tensor(h8[:, 4 * a:4 * a + 4, HD * h:HD * h + HD], back[:, a, :, 0:HD],
                                          rc[:, a, :].unsqueeze(2).to_broadcast([P, 4, HD]),
                                          ALU.mult).then_inc(o8_ready, 1)

                for i in range(NT):
                    dve.wait_ge(yhi_ready, it * NT + i + 1)
                    dve.tensor_tensor(y_lo[:, i % 2].rearrange("p k n -> p (k n)"), slots.tensors[slots.slot["y_t", i]][:, 0, 0:D],
                                      y_hi[:, i % 2].rearrange("p k n -> p (k n)").bitcast(F32),
                                      ALU.subtract).then_inc(y_ready, 1)
                    ps = filled(dve, it, "wo", i)
                    if i >= 2:
                        dve.wait_ge(x2_ready, it * NT + i - 1)
                    dve.tensor_tensor(yb[:, i % 2, :], ps[:, 0, 0:D], w["bo"][:, :], ALU.add).then_inc(yb_ready, 1)
                dve.wait_ge(x2_ready, (it + 1) * NT)
                layer_norm(x8, h8)
                link(dve.tensor_tensor(h8[:, :, :], h8[:, :, :], row(4), ALU.mult))
                dve.tensor_tensor(h8[:, :, :], h8[:, :, :], row(3), ALU.add).then_inc(h0_ready, 1)
                assert link.n - base == LINKS, link.n - base

        @block.tensor
        def _(pe):
            pe.wait_ge(preset, 2)
            hi, lo, ident = w["hi"], w["lo"], w["ident"]
            with pe.Fori(0, B) as it:
                def x_transpose(i):
                    ps = fill(pe, it, "x_t", i)
                    pe.wait_ge(xn_ready, it * NT + i + 1)
                    for k in range(KC):
                        last = pe.transpose(ps[:, 0, P * k:P * k + P], h8[:, i, P * k:P * k + P], ident[:, :])
                    last.then_inc(done["x_t"], 1)

                def qkv(i):
                    ps = fill(pe, it, "qkv", i)
                    pe.wait_ge(xt_ready, it * NT + i + 1)
                    a = [(x_hi[:, i % 2, k, :], x_lo[:, i % 2, k, :]) for k in range(KC)]
                    split3(pe, ps[:, 0, :], a, [(hi[:, k, 0:512], lo[:, k, 0:512]) for k in range(KC)])
                    split3(pe, ps[:, 1, 0:D], a, [(hi[:, k, 512:768], lo[:, k, 512:768]) for k in range(KC)]).then_inc(done["qkv"], 1)

                for i in range(NT + 1):
                    if i < NT:
                        x_transpose(i)
                    if i >= 1:
                        qkv(i - 1)
                for i in range(NT):
                    ps = fill(pe, it, "qk_t", i)
                    pe.wait_ge(s_ready, 2 * (it * NT + i) + 2)
                    for h in range(GH):
                        pe.transpose(ps[:, 0, P * h:P * h + P], q_s[:, i, h, 0:P].bitcast(F32), ident[:, :])
                    for h in range(GH):
                        last = pe.transpose(ps[:, 1, P * h:P * h + P], k_s[:, i % 2, h, 0:P].bitcast(F32), ident[:, :])
                    last.then_inc(done["qk_t"], 1)
                    ps = fill(pe, it, "kl_t", i)
                    for h in range(GH):
                        last = pe.transpose(ps[:, 0, P * h:P * h + P], k_s[:, i % 2, h, P:2 * P].bitcast(F32), ident[:, :])
                    last.then_inc(done["kl_t"], 1)

                def maxima(h, i):
                    ps = fill(pe, it, "max", NT * h + i)
                    for a in range(2):
                        last = pe.matmul(ps[:, a, :], q1[:, h, P * i:P * i + P], k1[:, h, HALF * a:HALF * a + HALF],
                                         start=True, stop=True)
                    last.then_inc(done["max"], 1)

                def max_transpose(h):
                    ps = fill(pe, it, "m_t", h)
                    pe.wait_ge(m_ready, it * GH + h + 1)
                    for i in range(NT):
                        last = pe.transpose(ps[:, i // 4, P * (i % 4):P * (i % 4) + P],
                                            q_s[:, i, h, HD:3 * HD].bitcast(F32), ident[:, :])
                    last.then_inc(done["m_t"], 1)

                for ready in (q1_ready, k1_ready, k2_ready):
                    pe.wait_ge(ready, NT * (it + 1))
                for i in range(NT):
                    maxima(0, i)
                max_transpose(0)

                def values(h, i):
                    n = h * NT + i
                    pe.wait_ge(p_ready, it * GH * NT + n + 1)
                    for a in range(2):
                        last = pe.matmul(slots.tensors["O"][0:HD + 1, a, :], v1[:, i, h, :], pr[:, n % 3, HALF * a:HALF * a + HALF],
                                         start=(i == 0), stop=(i == NT - 1))
                    last.then_inc(p_used, 1)

                for h in range(GH):
                    pe.wait_ge(q2_ready, it * GH + h + 1)
                    fill(pe, it, "out", h)
                    for i in range(NT):
                        ps = fill(pe, it, "s_t", NT * h + i)
                        for a in range(2):
                            cols = slice(HALF * a, HALF * a + HALF)
                            pe.matmul(ps[:, a, :], k1[:, h, P * i:P * i + P], q1[:, h, cols], start=True, stop=False)
                            last = pe.matmul(ps[:, a, :], k2[:, h, P * i:P * i + P], q2[:, h % 2, cols], start=False, stop=True)
                        last.then_inc(done["s_t"], 1)
                        if h + 1 < GH:
                            maxima(h + 1, i)
                        if i >= 1:
                            values(h, i - 1)
                    values(h, NT - 1)
                    if h + 1 < GH:
                        max_transpose(h + 1)
                    ps = fill(pe, it, "back", h)
                    pe.wait_ge(ot_ready, it * GH + h + 1)
                    for i in range(NT):
                        last = pe.transpose(ps[:, i // 4, P * (i % 4):P * (i % 4) + HD + 1],
                                            o_t[:, P * i:P * i + P], ident[0:HD + 1, 0:HD + 1])
                    last.then_inc(done["back"], 1)

                pe.wait_ge(o8_ready, 2 * GH * (it + 1))

                def y_transpose(i):
                    ps = fill(pe, it, "y_t", i)
                    for k in range(KC):
                        last = pe.transpose(ps[:, 0, P * k:P * k + P], h8[:, i, P * k:P * k + P], ident[:, :])
                    last.then_inc(done["y_t"], 1)

                for i in range(NT):
                    y_transpose(i)
                    ps = fill(pe, it, "wo", i)
                    pe.wait_ge(y_ready, it * NT + i + 1)
                    a = [(y_hi[:, i % 2, k, :], y_lo[:, i % 2, k, :]) for k in range(KC)]
                    split3(pe, ps[:, 0, 0:D], a, [(hi[:, k, 768:1024], lo[:, k, 768:1024]) for k in range(KC)]).then_inc(done["wo"], 1)


LH = 8
INNER = LH * HD
PAIRS = LH // 2
HID = D * 4 * 2 // 3
NL = 2
TURNS = NT // 2
NC = -(-HID // P)
CS = [HID // NC + (j < HID % NC) for j in range(NC)]
CO = [sum(CS[:j]) for j in range(NC)]
BIG = -1e30
NORM_EPS = 1e-12
QK_SCALE = 8.0


class Step:

    def __init__(self, l, tp, p):
        self.tp, self.p, self.u = tp, p, l * TURNS + tp

    def i(self, b):
        return B * self.p + b

    def n(self, b):
        return self.u * 2 * B + B * self.p + b


def layers_block(nc, io, scratch, out, ident):
    with ExitStack() as ctx:
        def sb(name, shape, dt=F32):
            return ctx.enter_context(nc.sbuf_tensor(f"l_{name}", shape, dt))

        def sem(name):
            return ctx.enter_context(nc.semaphore(f"l_{name}"))

        wqkv = [sb(f"wqkv_{s}", [P, KC, 3 * INNER], F32R) for s in ("hi", "lo")]
        wo = [sb(f"wo_{s}", [P, PAIRS, D], F32R) for s in ("hi", "lo")]
        w1 = [sb(f"w1_{s}", [P, KC, 2 * HID], F32R) for s in ("hi", "lo")]
        w2 = [sb(f"w2_{s}", [P, NC, D], F32R) for s in ("hi", "lo")]
        scales = sb("scales", [P, 4, HD])
        gb = sb("gb", [P, 2, KC])
        b1 = sb("b1", [P, 2 * NC])
        b2 = sb("b2", [P, D])
        gate = sb("gate", [P, B, D])
        flag = sb("flag", [P, 1])
        xs = sb("xs", [P, 2, B, 3, P])
        h_hi = sb("h_hi", [P, 2, KC, P], F32R)
        h_lo = sb("h_lo", [P, 2, KC, P], F32R)
        qk = sb("qk", [P, 2, 2 * LH, HD])
        t1 = sb("t1", [P, 2 * LH, HD])
        t2 = sb("t2", [P, 2 * LH, HD])
        ss = sb("ss", [P, 2 * LH])
        ra = sb("ra", [P, 2 * LH])
        rn = sb("rn", [P, B, 2 * LH])
        tab_in = sb("tab_in", [P, 4, HD])
        tab = sb("tab", [P, 2, 4, HD])
        mask = sb("mask", [P, 2, 2 * P])
        qt = sb("qt", [P, 2, LH, P])
        kt = sb("kt", [P, B, PAIRS, 2, P])
        vt = sb("vt", [P, B, 2, INNER])
        sm = sb("sm", [P, 4, 2, 2 * P])
        pt = sb("pt", [P, 2, 4, P])
        mx = sb("mx2", [P, 4, 2])
        nb = sb("nb", [P, 4, 2])
        rsum = sb("rsum", [P, 4, 2])
        rinv = sb("rinv", [P, 4, 2])
        o_hi = sb("o_hi", [P, 2, PAIRS, P], F32R)
        o_lo = sb("o_lo", [P, 2, PAIRS, P], F32R)
        st = sb("st2", [P, 6])
        mv = sb("mv2", [P, 2])
        rs = sb("rs2", [P, 1])
        var = sb("var2", [P, 1])
        tmp = sb("tmp2", [P, 1])
        xn = sb("xn", [P, 2, D])
        f_hi = sb("f_hi", [P, KC, B * P], F32R)
        f_lo = sb("f_lo", [P, KC, B * P], F32R)
        ge = sb("ge", [P, 2, B * P])
        up = sb("up", [P, 3, B * P])
        u_hi = sb("u_hi", [P, 2, B * P], F32R)
        u_lo = sb("u_lo", [P, 2, B * P], F32R)
        yb = sb("yb2", [P, B, D])
        base = sb("base", [P, B, D])
        stage = [qk[:, :, :, :].rearrange("p a h d -> p (a h d)"), sm[:, :, :, :].rearrange("p a b n -> p (a b n)")]

        banks = {s: ctx.enter_context(nc.psum_tensor(f"bank_{s}", [P, 512], F32))
                 for s in ("P0", "P1", "T0", "T1", "S0", "S1", "O0", "O1")}

        LAG = 3
        ROUNDS = B * PAIRS + 10

        def at(r, offset, every=PAIRS):
            b, rest = divmod(r - offset, every)
            return b if rest == 0 and 0 <= b < B else None

        order, ahead, count = [], [], {}
        rings = {"T": 0, "P": 0}

        def use(kind, ring, next_turn=False):
            i = count.get(kind, 0)
            count[kind] = i + 1
            if ring in rings:
                slot = f"{ring}{rings[ring] % 2}"
                rings[ring] += 1
            else:
                slot = ring
            order.append([kind, i, slot])
            if next_turn:
                ahead.append(order[-1])

        for p in range(2):
            def a_qkv(following=False):
                for kind in ("qk", "qk", "v"):
                    use(kind, "P", following and p == 1)

            for r in range(ROUNDS):
                if r < B * PAIRS:
                    use("s", f"S{r % 2}")
                if r in (0, PAIRS):
                    a_qkv()
                if 0 <= r - LAG < B * PAIRS:
                    use("p_t", "T")
                if 0 <= r - LAG - 1 < B * PAIRS and (r - LAG - 1) % PAIRS == 0:
                    use("o", f"O{(r - LAG - 1) // PAIRS % 2}")
                if r < B * PAIRS and r % PAIRS == 2 and r // PAIRS + 1 < B:
                    use("q_t", "T")
                    use("k_t", "T")
                if r == 3:
                    use("h_t", "T")
                if at(r, 8) is not None:
                    use("wo", "P")
                if at(r, 12) is not None:
                    use("x_t", "T")
                if r == 18:
                    use("h_t", "T", p == 1)
                    use("h_t", "T", p == 1)
                if r in (19, 21):
                    a_qkv(True)
                if r == 20:
                    use("h_t", "T", p == 1)
            for j in range(NC + 2):
                if j < NC:
                    use("g", ("P0", "S0")[j % 2])
                    use("a", ("P1", "S1")[j % 2])
                if j == 2:
                    use("q_t", "T", p == 1)
                    use("k_t", "T", p == 1)
                    use("y", "O0")
                    use("y", "O1")
        shift = {}
        for entry in ahead:
            shift[entry[0]] = shift.get(entry[0], 0) + 1
        for entry in order:
            entry[1] = (entry[1] + shift.get(entry[0], 0)) % count[entry[0]]
        ahead = [(k, i) for k, i, _ in ahead]

        done = {k: sem(f"{k}_done2") for k in count if k not in ("o", "y")}
        pv_done = sem("pv_done")
        w2_done = sem("w2_done")
        done["o"], done["y"] = pv_done, w2_done
        w_loaded = [sem("w_loaded0"), sem("w_loaded1")]
        par_loaded = sem("par_loaded")
        w_hi = sem("w_hi")
        w_lo = sem("w_lo")
        bias_done = sem("bias_done")
        waited_pool, waited_dve, waited_pe, waited_sp = (sem(f"waited_{e}") for e in ("pool", "dve", "pe", "sp"))
        preset = sem("preset2")
        xs_loaded = [[sem(f"xs_loaded{p}{b}") for b in range(B)] for p in range(2)]
        base_loaded = [sem(f"base_loaded{b}") for b in range(B)]
        mask_loaded = sem("mask_loaded")
        tab_loaded = sem("tab_loaded")
        tab_ready = sem("tab_ready")
        hhi_ready = sem("hhi_ready")
        h_ready = sem("h_ready")
        qk_ready = sem("qk_ready2")
        v_ready = sem("v_ready2")
        sq_ready = sem("sq_ready2")
        sq_used = sem("sq_used2")
        t1_ready = sem("t1_ready")
        t2_ready = sem("t2_ready")
        rot_ready = sem("rot_ready")
        qt_ready = sem("qt_ready")
        kt_ready = sem("kt_ready")
        sm_ready = sem("sm_ready")
        nb_ready = sem("nb_ready")
        ex_ready = sem("ex_ready")
        ri_ready = sem("ri_ready")
        pn_ready = sem("pn_ready")
        pt_ready = sem("pt_ready")
        ohi_ready = sem("ohi_ready")
        o_ready = sem("o_ready")
        x1_ready = sem("x1_ready")
        x1_stored = sem("x1_stored")
        sh_loaded = [sem(f"sh_loaded{b}") for b in range(B)]
        xn_ready = [sem(f"xn_ready{p}") for p in range(2)]
        xb_ready = [sem(f"xb_ready{p}") for p in range(2)]
        fhi_ready = sem("fhi_ready")
        f_ready = sem("f_ready")
        ge_ready = sem("ge_ready")
        up_ready = sem("up_ready")
        uhi_ready = sem("uhi_ready")
        u_ready = sem("u_ready")
        y_ready = sem("y_ready2")
        gy_ready = sem("gy_ready")
        y2_ready = sem("y2_ready")
        y_stored = [sem(f"y_stored{b}") for b in range(B)]
        o_stored = [sem(f"o_stored{b}") for b in range(B)]
        chain_w = sem("chain_w")
        chain = sem("chain2")
        slots = Slots(order, banks, done, {
            "h_t": [(h_ready, 1)], "qk": [(qk_ready, 1)], "v": [(v_ready, 1)], "q_t": [(qt_ready, 2)],
            "k_t": [(kt_ready, 1)], "s": [(sm_ready, 2)], "p_t": [(pt_ready, 1)], "o": [(o_ready, 1)],
            "wo": [(x1_ready, 1)], "x_t": [(f_ready, 1)], "a": [(up_ready, 1)], "g": [(ge_ready, 1)],
            "y": [(y_ready, 2)]}, ahead)
        fill, filled = slots.fill, slots.filled
        STAGED = 6
        block = ctx.enter_context(nc.Block())

        @block.sync
        def _(sp):
            for b in range(B):
                sp.sem_inc(y_stored[b], 16 * NT)
            with sp.Fori(0, NL) as l:
                def row(name):
                    return io[name][bass.ds(l, 1)]

                for b in range(B):
                    sp.wait_ge(y_stored[b], 16 * NT * (l + 1))
                for i, (name, cut) in enumerate((("q_scale", 0), ("k_scale", 0))):
                    sp.dma_start(scales[:, 2 * i, :], row(name).to_broadcast([P, HD])).then_inc(par_loaded, 16)
                    sp.dma_start(scales[:, 2 * i + 1, 0:HD // 2], row(name)[:, HD // 2:HD].to_broadcast([P, HD // 2])).then_inc(par_loaded, 16)
                    sp.dma_start(scales[:, 2 * i + 1, HD // 2:HD], row(name)[:, 0:HD // 2].to_broadcast([P, HD // 2])).then_inc(par_loaded, 16)
                with nc.allow_non_contiguous_dma(reason="parameters by feature, a column each"):
                    for i, name in enumerate(("lg", "lb")):
                        sp.dma_start(gb[:, i, :], row(name).rearrange("a (k p) -> p (a k)", k=KC)).then_inc(par_loaded, 16)
                    for g in range(2):
                        for j in range(NC):
                            sp.dma_start(b1[0:CS[j], NC * g + j:NC * g + j + 1],
                                         row("b1")[:, HID * g + CO[j]:HID * g + CO[j] + CS[j]].rearrange("a p -> p a")).then_inc(par_loaded, 16)
                sp.dma_start(b2[:, :], row("b2").to_broadcast([P, D])).then_inc(par_loaded, 16)
                sp.dma_start(flag[:, :], row("flags").to_broadcast([P, 1])).then_inc(par_loaded, 16)
                sp.dma_start(gate[:, :, :].rearrange("p b d -> p (b d)"),
                             scratch["gate"][bass.ds(l, 1)].rearrange("a b d -> a (b d)").to_broadcast([P, B * D])).then_inc(par_loaded, 16)
                wq_v = row("wqkv").rearrange("a (k p) n -> p (a k) n", k=KC)
                w1_v = row("w1").rearrange("a (k p) n -> p (a k) n", k=KC)
                for i in range(STAGED):
                    if i >= 2:
                        sp.wait_ge(w_lo, STAGED * l + i - 1)
                    s = stage[i % 2]
                    if i < 2:
                        pairs = [(s[:, 0:3 * INNER], wq_v[:, i, :])]
                    elif i == 2:
                        pairs = [(s[:, 0:PAIRS * D].rearrange("p (c n) -> p c n", c=PAIRS),
                                  row("f_wo").rearrange("a (c p) n -> p (a c) n", c=PAIRS))]
                    elif i < 5:
                        pairs = [(s[:, 0:2 * HID], w1_v[:, i - 3, :])]
                    else:
                        n = CS.count(CS[0])
                        v = s[:, 0:NC * D].rearrange("p (c n) -> p c n", c=NC)
                        pairs = [(v[0:CS[0], 0:n, :], row("w2")[:, 0:CO[n], :].rearrange("a (c p) n -> p (a c) n", c=n)),
                                 (v[0:CS[-1], n:NC, :], row("w2")[:, CO[n]:HID, :].rearrange("a (c p) n -> p (a c) n", c=NC - n))]
                    for dst, src in pairs:
                        sp.dma_start(dst, src).then_inc(w_loaded[i % 2], 16)

                def load(s):
                    t, step = s.tp * 2 + s.p, s.u * 2 + s.p
                    sp.wait_ge(tab_ready, step)
                    sp.dma_start(tab_in[:, :, :], io["rope"][bass.ds(t, 1)].rearrange("a p c d -> p (a c) d")).then_inc(tab_loaded, 16)
                    for b in range(B):
                        sp.wait_ge(xn_ready[s.p], B * s.u)
                        sp.wait_ge(xb_ready[s.p], B * s.u)
                        sp.wait_ge(y_stored[b], 16 * (step + 1))
                        src = scratch["x"][bass.ds(l, 1), b]
                        sp.dma_start(xs[:, s.p, b, 0:3:2, :],
                                     src[:, bass.ds(t * P + 1, P), :].rearrange("a p (c n) -> p (a c) n", c=2)).then_inc(xs_loaded[s.p][b], 16)
                        sp.dma_start(xs[:, s.p, b, 1, :],
                                     src[:, bass.ds(t * P, P), P:D].rearrange("a p n -> p (a n)")).then_inc(xs_loaded[s.p][b], 16)

                def load_mask(s):
                    sp.wait_ge(sm_ready, s.u * 2 * 2 * B * PAIRS)
                    sp.dma_start(mask[:, :, :], io["mask"][bass.ds(s.tp, 1)].rearrange("a p c n -> p (a c) n")).then_inc(mask_loaded, 16)

                def step(s, following):
                    t, step = s.tp * 2 + s.p, s.u * 2 + s.p
                    for b in range(B):
                        sp.wait_ge(y2_ready, B * step)
                        stand_alone(sp, waited_sp)
                        sp.dma_start(base[:, b, :], scratch["base"][b, bass.ds(t * P, P), :]).then_inc(base_loaded[b], 16)
                    if following:
                        load(following)
                    for b in range(B):
                        sp.wait_ge(x1_ready, B * step + b + 1)
                        stand_alone(sp, waited_sp)
                        sp.dma_start(scratch["xa"][b, bass.ds(t * P + 1, P), :].rearrange("p (c n) -> p c n", c=2),
                                     xs[:, s.p, b, 0:3:2, :]).then_inc(x1_stored, 16)
                        sp.wait_ge(x1_stored, 16 * (B * step + b + 1))
                        sp.dma_start(xs[:, s.p, b, 1, :], scratch["xa"][b, bass.ds(t * P, P), P:D]).then_inc(sh_loaded[b], 16)
                    if following and following.p == 0:
                        load_mask(following)
                    for b in range(B):
                        sp.wait_ge(y2_ready, B * step + b + 1)
                        stand_alone(sp, waited_sp)
                        sp.dma_start(scratch["x"][bass.ds(l + 1, 1), b, bass.ds(t * P + 1, P), :].rearrange("a p n -> p (a n)"),
                                     yb[:, b, :]).then_inc(y_stored[b], 16)
                        sp.wait_ge(o_stored[b], 16 * step)
                        sp.dma_start(out[b, bass.ds(t * P, P), :], yb[:, b, :]).then_inc(o_stored[b], 16)

                load(Step(l, 0, 0))
                load_mask(Step(l, 0, 0))
                with sp.Fori(0, TURNS - 1) as tp:
                    step(Step(l, tp, 0), Step(l, tp, 1))
                    step(Step(l, tp, 1), Step(l, tp + 1, 0))
                step(Step(l, TURNS - 1, 0), Step(l, TURNS - 1, 1))
                step(Step(l, TURNS - 1, 1), None)
            for b in range(B):
                sp.wait_ge(y_stored[b], 16 * NT * (NL + 1))
                sp.wait_ge(o_stored[b], 16 * NT * NL)

        @block.gpsimd
        def _(pool):
            pool.memset(qt[:, :, :, :], 0.0).then_inc(preset, 1)
            pool.memset(kt[:, :, :, :, :], 0.0).then_inc(preset, 1)
            pool.memset(vt[:, :, :, :], 0.0).then_inc(preset, 1)
            PAR = 16 * (6 + 2 + 2 * NC + 3)
            with pool.Fori(0, NL) as l:
                pool.wait_ge(par_loaded, PAR * (l + 1))
                stand_alone(pool, waited_pool)
                def tables(s):
                    pool.wait_ge(tab_loaded, 16 * (2 * s.u + s.p + 1))
                    pool.wait_ge(t1_ready, s.u * 2 * B)
                    pool.tensor_tensor(tab[:, s.p], tab_in[:, :, :], scales[:, :, :], ALU.mult).then_inc(tab_ready, 1)

                def rotate(s, b):
                    n = s.n(b)
                    pool.wait_ge(tab_ready, 2 * s.u + s.p + 1)
                    pool.wait_ge(sq_used, n + 1)
                    pool.wait_ge(qk_ready, 2 * n + 2)
                    src = qk[:, b % 2].rearrange("p (a h) d -> p a h d", a=2)
                    dst = t2[:, :, :].rearrange("p (a h) d -> p a h d", a=2)
                    H2 = HD // 2
                    for lo, hi in ((0, H2), (H2, 0)):
                        for a in range(2):
                            pool.tensor_tensor(dst[:, a, :, lo:lo + H2], src[:, a, :, hi:hi + H2],
                                               tab[:, s.p, 2 * a + 1, lo:lo + H2].unsqueeze(1).to_broadcast([P, LH, H2]),
                                               ALU.mult).then_inc(t2_ready, 1)

                def probabilities(s, r):
                    n = (2 * s.u + s.p) * B * PAIRS + r
                    pool.wait_ge(ri_ready, n + 1)
                    pool.tensor_tensor(sm[:, r % 4], sm[:, r % 4],
                                       rinv[:, r % 4, :].unsqueeze(2).to_broadcast([P, 2, 2 * P]),
                                       ALU.mult).then_inc(pn_ready, 1)

                def x_bias(s, b):
                    pool.wait_ge(x1_ready, s.n(b) + 1)
                    pool.wait_ge(y_stored[b], 16 * (NT + 2 * s.u + s.p))
                    pool.wait_ge(o_stored[b], 16 * (2 * s.u + s.p))
                    pool.tensor_tensor(yb[:, b, :].rearrange("p (c n) -> p c n", c=2), xs[:, s.p, b, 0:3:2, :],
                                       b2[:, :].rearrange("p (c n) -> p c n", c=2), ALU.add).then_inc(xb_ready[s.p], 1)

                def ahead(s):
                    tables(s)
                    rotate(s, 0)

                def step(s, following):
                    for r in range(ROUNDS):
                        if 1 <= r <= B * PAIRS:
                            probabilities(s, r - 1)
                        if r in (0, 3, 7):
                            rotate(s, {0: 1, 3: 2, 7: 3}[r])
                        if (b := at(r, 11)) is not None:
                            x_bias(s, b)
                        if r == 20 and following:
                            ahead(following)
                    for j in range(NC):
                        m = (2 * s.u + s.p) * NC + j
                        pool.wait_ge(uhi_ready, m + 1)
                        if NC * s.p + j >= 2:
                            pool.wait_ge(w2_done, B * (m - 1))
                        pool.tensor_tensor(u_lo[0:CS[j], j % 2, :], up[0:CS[j], j % 3, :],
                                           u_hi[0:CS[j], j % 2, :].bitcast(F32), ALU.subtract).then_inc(u_ready, 1)
                    for b in range(B):
                        pool.wait_ge(y_ready, s.n(b) + 1)
                        pool.tensor_tensor(yb[:, b, :], yb[:, b, :], gate[:, b, :], ALU.mult).then_inc(gy_ready, 1)

                slots.phase = "first"
                ahead(Step(l, 0, 0))
                slots.phase = "body"
                with pool.Fori(0, TURNS - 1) as tp:
                    step(Step(l, tp, 0), Step(l, tp, 1))
                    step(Step(l, tp, 1), Step(l, tp + 1, 0))
                slots.phase = "last"
                step(Step(l, TURNS - 1, 0), Step(l, TURNS - 1, 1))
                step(Step(l, TURNS - 1, 1), None)

        @block.scalar
        def _(act):
            PAR = 16 * (6 + 2 + 2 * NC + 3)
            with act.Fori(0, NL) as l:
                act.wait_ge(par_loaded, PAR * (l + 1))
                loads = [0, 0]
                per_stage = [3, 4]
                for i in range(STAGED):
                    loads[i % 2] += 2 if i == 5 else 1
                    act.wait_ge(w_loaded[i % 2], 16 * (per_stage[i % 2] * l + loads[i % 2]))
                    s = stage[i % 2]
                    if i < 2:
                        act.copy(wqkv[0][:, i, :], s[:, 0:3 * INNER]).then_inc(w_hi, 1)
                    elif i == 2:
                        act.copy(wo[0][:, :, :].rearrange("p c n -> p (c n)"), s[:, 0:PAIRS * D]).then_inc(w_hi, 1)
                    elif i < 5:
                        act.activation(w1[0][:, i - 3, :], s[:, 0:2 * HID], ACT.Copy, scale=gb[:, 0, i - 3:i - 2]).then_inc(w_hi, 1)
                    else:
                        n = CS.count(CS[0])
                        v = s[:, 0:NC * D].rearrange("p (c n) -> p c n", c=NC)
                        act.copy(w2[0][0:CS[0], 0:n, :], v[0:CS[0], 0:n, :]).then_inc(w_hi, 1)
                        act.copy(w2[0][0:CS[-1], n:NC, :], v[0:CS[-1], n:NC, :]).then_inc(w_hi, 1)
                def h_out(s, b):
                    ps = filled(act, s.u, "h_t", s.i(b))
                    if s.i(b) >= 2:
                        filled(act, s.u, "v", s.i(b) - 2)
                    act.copy(h_hi[:, b % 2].rearrange("p k n -> p (k n)"), ps[:, 0:D]).then_inc(hhi_ready, 1)

                def qkv_out(s, b):
                    if s.i(b) >= 2:
                        filled(act, s.u, "k_t", s.i(b) - 2)
                    for a in range(2):
                        ps = filled(act, s.u, "qk", 2 * s.i(b) + a)
                        act.copy(qk[:, b % 2, LH * a:LH * a + LH, :].rearrange("p h d -> p (h d)"), ps[:, :]).then_inc(qk_ready, 1)
                    ps = filled(act, s.u, "v", s.i(b))
                    act.copy(vt[:, b, s.p, :], ps[:, :]).then_inc(v_ready, 1)

                def squares(s, b):
                    n = s.n(b)
                    act.wait_ge(qk_ready, 2 * n + 2)
                    act.wait_ge(rot_ready, n)
                    act.activation(t2[:, :, :], qk[:, b % 2], ACT.Square).then_inc(sq_ready, 1)

                def k_out(s, b):
                    ps = filled(act, s.u, "k_t", s.i(b))
                    act.copy(kt[:, b, :, s.p, :], ps[:, :].rearrange("p (c n) -> p c n", c=PAIRS)).then_inc(kt_ready, 1)

                def exps(s, r):
                    n = (2 * s.u + s.p) * B * PAIRS + r
                    act.wait_ge(nb_ready, n + 1)
                    for e in range(2):
                        act.activation(sm[:, r % 4, e, :], sm[:, r % 4, e, :], ACT.Exp, bias=nb[:, r % 4, e:e + 1],
                                       scale=rn[:, r // PAIRS, 2 * (r % PAIRS) + e:2 * (r % PAIRS) + e + 1],
                                       accum_out=rsum[:, r % 4, e:e + 1]).then_inc(ex_ready, 1)

                def pt_out(s, r):
                    ps = filled(act, s.u, "p_t", B * PAIRS * s.p + r)
                    n = (2 * s.u + s.p) * B * PAIRS + r
                    if B * PAIRS * s.p + r >= 2:
                        act.wait_ge(pv_done, n - 1)
                    act.copy(pt[:, r % 2].rearrange("p c n -> p (c n)"), ps[:, :]).then_inc(pt_ready, 1)

                def o_out(s, b):
                    act.wait_ge(pv_done, (s.n(b) + 1) * PAIRS)
                    if s.i(b) >= 2:
                        filled(act, s.u, "wo", s.i(b) - 2)
                    act.copy(o_hi[:, b % 2].rearrange("p c n -> p (c n)"), banks[f"O{b % 2}"][:, :]).then_inc(ohi_ready, 1)

                def f_out(s, b):
                    ps = filled(act, s.u, "x_t", s.i(b))
                    act.copy(f_hi[:, :, P * b:P * b + P], ps[:, 0:D].rearrange("p (k n) -> p k n", k=KC)).then_inc(fhi_ready, 1)

                def gelu(s, j):
                    m = (2 * s.u + s.p) * NC + j
                    ps = filled(act, s.u, "g", NC * s.p + j)
                    if NC * s.p + j >= 2:
                        act.wait_ge(up_ready, m - 1)
                    act.activation(ge[0:CS[j], j % 2, :], ps[0:CS[j], :], ACT.Gelu,
                                   bias=b1[0:CS[j], NC + j:NC + j + 1]).then_inc(ge_ready, 1)

                def u_split(s, j):
                    m = (2 * s.u + s.p) * NC + j
                    act.wait_ge(up_ready, m + 1)
                    if NC * s.p + j >= 2:
                        act.wait_ge(w2_done, B * (m - 1))
                    act.copy(u_hi[0:CS[j], j % 2, :], up[0:CS[j], j % 3, :]).then_inc(uhi_ready, 1)

                def ahead(s, part):
                    if part == 0:
                        h_out(s, 0), h_out(s, 1)
                    elif part == 1:
                        qkv_out(s, 0), squares(s, 0)
                    elif part == 2:
                        h_out(s, 2), qkv_out(s, 1)
                    elif part == 3:
                        squares(s, 1)
                    else:
                        k_out(s, 0)

                def step(s, following):
                    for r in range(ROUNDS):
                        b, j = divmod(r, PAIRS)
                        if b < B:
                            exps(s, r)
                        if r in (0, PAIRS):
                            qkv_out(s, b + 2), squares(s, b + 2)
                        if 0 <= r - LAG < B * PAIRS:
                            pt_out(s, r - LAG)
                        if b + 1 < B and j == 2:
                            k_out(s, b + 1)
                        if r == 3:
                            h_out(s, 3)
                        if (b := at(r, 7)) is not None:
                            o_out(s, b)
                        if (b := at(r, 12)) is not None:
                            f_out(s, b)
                        if following and r in (18, 19, 21):
                            ahead(following, {18: 0, 19: 1, 21: 2}[r])
                    for j in range(NC + 1):
                        if j < NC:
                            gelu(s, j)
                        if j >= 1:
                            u_split(s, j - 1)
                        if following and j in (0, 3):
                            ahead(following, {0: 3, 3: 4}[j])

                slots.phase = "first"
                for part in range(5):
                    ahead(Step(l, 0, 0), part)
                slots.phase = "body"
                with act.Fori(0, TURNS - 1) as tp:
                    step(Step(l, tp, 0), Step(l, tp, 1))
                    step(Step(l, tp, 1), Step(l, tp + 1, 0))
                slots.phase = "last"
                step(Step(l, TURNS - 1, 0), Step(l, TURNS - 1, 1))
                step(Step(l, TURNS - 1, 1), None)

        LINKS_W = 1 + 2 * KC
        LINKS = 2 * B * ((3 + RSQRT_LINKS) + 2 + (3 + RSQRT_LINKS))
        LINKS_AHEAD = 2 * (3 + RSQRT_LINKS) + 2

        @block.vector
        def _(dve):
            PAR = 16 * (6 + 2 + 2 * NC + 3)
            dve.wait_ge(preset, 3)
            link_w, link = Link(dve, chain_w, LINKS_W), Link(dve, chain, LINKS)
            with dve.Fori(0, NL) as l:
                link_w.turn, link_w.n = l, 0
                dve.wait_ge(par_loaded, PAR * (l + 1))
                for i in range(STAGED):
                    dve.wait_ge(w_hi, (STAGED + 1) * l + i + 1 + (i == 5))
                    s = stage[i % 2]
                    if i < 2:
                        dve.tensor_tensor(wqkv[1][:, i, :], s[:, 0:3 * INNER], wqkv[0][:, i, :].bitcast(F32),
                                          ALU.subtract).then_inc(w_lo, 1)
                    elif i == 2:
                        dve.tensor_tensor(wo[1][:, :, :].rearrange("p c n -> p (c n)"), s[:, 0:PAIRS * D],
                                          wo[0][:, :, :].rearrange("p c n -> p (c n)").bitcast(F32), ALU.subtract).then_inc(w_lo, 1)
                    elif i < 5:
                        dve.wait_ge(bias_done, KC * l + i - 2)
                        dve.scalar_tensor_tensor(out=w1[1][:, i - 3, :], in0=s[:, 0:2 * HID], scalar=gb[:, 0, i - 3:i - 2],
                                                 in1=w1[0][:, i - 3, :].bitcast(F32), op0=ALU.mult, op1=ALU.subtract).then_inc(w_lo, 1)
                    else:
                        n = CS.count(CS[0])
                        v = s[:, 0:NC * D].rearrange("p (c n) -> p c n", c=NC)
                        link_w(dve.tensor_tensor(w2[1][0:CS[0], 0:n, :], v[0:CS[0], 0:n, :], w2[0][0:CS[0], 0:n, :].bitcast(F32), ALU.subtract))
                        dve.tensor_tensor(w2[1][0:CS[-1], n:NC, :], v[0:CS[-1], n:NC, :], w2[0][0:CS[-1], n:NC, :].bitcast(F32),
                                          ALU.subtract).then_inc(w_lo, 1)
                n = CS.count(CS[0])
                b1_v = b1[:, :].rearrange("p (g c) -> p g c", g=2)
                for rows, c0, c1 in ((CS[0], 0, n), (CS[-1], n, NC)):
                    for k in range(KC):
                        link_w(dve.tensor_tensor(b1_v[0:rows, :, c0:c1], b1_v[0:rows, :, c0:c1],
                                                 banks[f"P{k}"][0:rows, 0:2 * NC].rearrange("p (g c) -> p g c", g=2)[:, :, c0:c1], ALU.add))
                link_w.wait()
                assert link_w.n == LINKS_W, link_w.n
                stand_alone(dve, waited_dve)

                def h_split(s, b):
                    dve.wait_ge(hhi_ready, s.n(b) + 1)
                    ps = banks[slots.slot["h_t", s.i(b)]]
                    dve.tensor_tensor(h_lo[:, b % 2].rearrange("p k n -> p (k n)"), ps[:, 0:D],
                                      h_hi[:, b % 2].rearrange("p k n -> p (k n)").bitcast(F32), ALU.subtract).then_inc(h_ready, 1)

                def norms(s, b):
                    n = s.n(b)
                    dve.wait_ge(sq_ready, n + 1)
                    dve.tensor_reduce(ss[:, :], t2[:, :, :], AX, ALU.add).then_inc(sq_used, 1)
                    dve.wait_ge(tab_ready, 2 * s.u + s.p + 1)
                    if s.i(b) >= 1:
                        filled(dve, s.u, "k_t", s.i(b) - 1)
                    for a in range(2):
                        ins = dve.tensor_tensor(t1[:, LH * a:LH * a + LH, :], qk[:, b % 2, LH * a:LH * a + LH, :],
                                                tab[:, s.p, 2 * a, :].unsqueeze(1).to_broadcast([P, LH, HD]), ALU.mult)
                        if a == 0:
                            link.done(ins)
                        else:
                            ins.then_inc(t1_ready, 1)
                    dve.wait_ge(sq_used, n + 1)
                    link(dve.tensor_scalar(ss[:, :], ss[:, :], NORM_EPS ** 2, None, ALU.max))
                    rsqrt(dve, link, rn[:, b, :], ss[:, :], ra[:, :])
                    link(dve.tensor_scalar(rn[:, b, 0:LH], rn[:, b, 0:LH], QK_SCALE, None, ALU.mult))

                def rotated(s, b):
                    n = s.n(b)
                    dve.wait_ge(t1_ready, n + 1)
                    dve.wait_ge(t2_ready, 4 * n + 4)
                    link(dve.tensor_tensor(t1[:, LH:, :], t1[:, LH:, :], t2[:, LH:, :], ALU.add))
                    link(dve.tensor_tensor(t1[:, LH:, :], t1[:, LH:, :],
                                           rn[:, b, LH:].unsqueeze(2).to_broadcast([P, LH, HD]), ALU.mult))
                    dve.tensor_tensor(t1[:, 0:LH, :], t1[:, 0:LH, :], t2[:, 0:LH, :], ALU.add).then_inc(rot_ready, 1)

                def q_out(s, b):
                    ps = filled(dve, s.u, "q_t", s.i(b))
                    for e in range(2):
                        rows = slice(HD * e, HD * e + HD)
                        dve.tensor_copy(qt[rows, b % 2, e:LH:2, :], ps[rows, :].rearrange("p (c n) -> p c n", c=PAIRS)).then_inc(qt_ready, 1)

                def maxima(s, r):
                    n = (2 * s.u + s.p) * B * PAIRS + r
                    ps = filled(dve, s.u, "s", B * PAIRS * s.p + r)
                    dve.wait_ge(mask_loaded, 16 * (s.u + 1))
                    if B * PAIRS * s.p + r >= 4:
                        filled(dve, s.u, "p_t", B * PAIRS * s.p + r - 4)
                    stand_alone(dve, waited_dve)
                    for e in range(2):
                        dve.tensor_tensor_reduce(sm[:, r % 4, e, :], ps[:, 2 * P * e:2 * P * e + 2 * P], mask[:, s.p, :], 1.0, -3.0e38,
                                                 ALU.add, ALU.max, mx[:, r % 4, e:e + 1]).then_inc(sm_ready, 1)
                    dve.wait_ge(sm_ready, 2 * n + 2)
                    h = 2 * (r % PAIRS)
                    dve.scalar_tensor_tensor(out=nb[:, r % 4, :], in0=mx[:, r % 4, :], scalar=-1.0,
                                             in1=rn[:, r // PAIRS, h:h + 2], op0=ALU.mult, op1=ALU.mult).then_inc(nb_ready, 1)

                def inverse(s, r):
                    n = (2 * s.u + s.p) * B * PAIRS + r
                    dve.wait_ge(ex_ready, 2 * n + 2)
                    dve.reciprocal(rinv[:, r % 4, :], rsum[:, r % 4, :]).then_inc(ri_ready, 1)

                def o_split(s, b):
                    dve.wait_ge(ohi_ready, s.n(b) + 1)
                    dve.tensor_tensor(o_lo[:, b % 2].rearrange("p c n -> p (c n)"), banks[f"O{b % 2}"][:, :],
                                      o_hi[:, b % 2].rearrange("p c n -> p (c n)").bitcast(F32), ALU.subtract).then_inc(o_ready, 1)

                def residual(s, b):
                    ps = filled(dve, s.u, "wo", s.i(b))
                    dve.tensor_tensor(xs[:, s.p, b, 0:3:2, :], ps[:, 0:D].rearrange("p (c n) -> p c n", c=2),
                                      xs[:, s.p, b, 0:3:2, :], ALU.add).then_inc(x1_ready, 1)

                def layer_norm(s, b):
                    dve.wait_ge(sh_loaded[b], 16 * (2 * s.u + s.p + 1))
                    dve.wait_ge(x1_ready, s.n(b) + 1)
                    link(dve.bn_stats(st[:, :], xs[:, s.p, b, 0:2, :]))
                    stand_alone(dve, waited_dve)
                    link(dve.bn_aggr(mv[:, :], st[:, :]))
                    link(dve.tensor_scalar(var[:, :], mv[:, 1:2], LN_EPS, None, ALU.add))
                    rsqrt(dve, link, rs[:, :], var[:, :], tmp[:, :])
                    if s.i(b) >= 2:
                        filled(dve, s.u, "x_t", s.i(b) - 2)
                    dve.tensor_scalar(xn[:, b % 2, :].rearrange("p (c n) -> p c n", c=2), xs[:, s.p, b, 0:2, :], mv[:, 0:1], rs[:, 0:1],
                                      ALU.subtract, ALU.mult).then_inc(xn_ready[s.p], 1)
                    dve.wait_ge(xn_ready[s.p], B * s.u + b + 1)

                def f_split(s, b):
                    dve.wait_ge(fhi_ready, s.n(b) + 1)
                    ps = banks[slots.slot["x_t", s.i(b)]]
                    dve.tensor_tensor(f_lo[:, :, P * b:P * b + P], ps[:, 0:D].rearrange("p (k n) -> p k n", k=KC),
                                      f_hi[:, :, P * b:P * b + P].bitcast(F32), ALU.subtract).then_inc(f_ready, 1)

                def up_out(s, j):
                    m = (2 * s.u + s.p) * NC + j
                    ps = filled(dve, s.u, "a", NC * s.p + j)
                    dve.wait_ge(ge_ready, m + 1)
                    if NC * s.p + j >= 3:
                        dve.wait_ge(u_ready, m - 2)
                    dve.scalar_tensor_tensor(out=up[0:CS[j], j % 3, :], in0=ps[0:CS[j], :], scalar=b1[0:CS[j], j:j + 1],
                                             in1=ge[0:CS[j], j % 2, :], op0=ALU.add, op1=ALU.mult).then_inc(up_ready, 1)

                def ahead(s, part):
                    if part == 0:
                        h_split(s, 0), h_split(s, 1)
                    elif part == 1:
                        norms(s, 0), h_split(s, 2)
                    elif part == 2:
                        rotated(s, 0)
                    elif part == 3:
                        norms(s, 1)
                    else:
                        q_out(s, 0)

                def step(s, following):
                    for r in range(ROUNDS):
                        b, j = divmod(r, PAIRS)
                        if b < B:
                            maxima(s, r)
                        if 1 <= r <= B * PAIRS:
                            inverse(s, r - 1)
                        if b + 1 < B and j == 0:
                            rotated(s, b + 1)
                        if b + 1 < B and j == 2:
                            q_out(s, b + 1)
                        if r == 3:
                            h_split(s, 3)
                        if b + 2 < B and j == 3:
                            norms(s, b + 2)
                        if (b := at(r, 7)) is not None:
                            o_split(s, b)
                        if (b := at(r, 9)) is not None:
                            residual(s, b)
                        if (b := at(r, 11)) is not None:
                            layer_norm(s, b)
                        if (b := at(r, 13)) is not None:
                            f_split(s, b)
                        if following and r in (18, 22):
                            ahead(following, {18: 0, 22: 1}[r])
                    for j in range(NC):
                        up_out(s, j)
                        if following and j in (0, 2, 4):
                            ahead(following, {0: 2, 2: 3, 4: 4}[j])
                    for b in range(B):
                        dve.wait_ge(w2_done, B * NC * (2 * s.u + s.p + 1))
                        dve.wait_ge(xb_ready[s.p], B * s.u + b + 1)
                        dve.tensor_tensor(yb[:, b, :], banks[f"O{b // 2}"][:, D * (b % 2):D * (b % 2) + D], yb[:, b, :],
                                          ALU.add).then_inc(y_ready, 1)
                    for b in range(B):
                        dve.wait_ge(gy_ready, s.n(b) + 1)
                        dve.wait_ge(base_loaded[b], 16 * (2 * s.u + s.p + 1))
                        dve.scalar_tensor_tensor(out=yb[:, b, :], in0=base[:, b, :], scalar=flag[:, 0:1], in1=yb[:, b, :],
                                                 op0=ALU.mult, op1=ALU.add).then_inc(y2_ready, 1)

                slots.phase = "first"
                link.turn, link.n = l * TURNS, 0
                for part in range(5):
                    ahead(Step(l, 0, 0), part)
                slots.phase = "body"
                with dve.Fori(0, TURNS - 1) as tp:
                    link.turn, link.n = l * TURNS + tp, LINKS_AHEAD
                    step(Step(l, tp, 0), Step(l, tp, 1))
                    step(Step(l, tp, 1), Step(l, tp + 1, 0))
                assert link.n == LINKS + LINKS_AHEAD, link.n
                slots.phase = "last"
                link.turn, link.n = l * TURNS + TURNS - 1, LINKS_AHEAD
                step(Step(l, TURNS - 1, 0), Step(l, TURNS - 1, 1))
                step(Step(l, TURNS - 1, 1), None)
                assert link.n == LINKS, link.n

        @block.tensor
        def _(pe):
            pe.wait_ge(preset, 3)
            with pe.Fori(0, NL) as l:
                pe.wait_ge(par_loaded, 16 * (6 + 2 + 2 * NC + 3) * (l + 1))
                for k in range(KC):
                    i = 3 + k
                    pe.wait_ge(w_loaded[i % 2], 16 * ([3, 4][i % 2] * l + [3, 2][i % 2]))
                    for g in range(2):
                        for j in range(NC):
                            c = HID * g + CO[j]
                            last = pe.matmul(banks[f"P{k}"][0:CS[j], NC * g + j:NC * g + j + 1], stage[i % 2][:, c:c + CS[j]],
                                             gb[:, 1, k:k + 1], start=True, stop=True)
                    last.then_inc(bias_done, 1)
                pe.wait_ge(w_lo, STAGED * (l + 1))
                pe.wait_ge(chain_w, LINKS_W * (l + 1))
                stand_alone(pe, waited_pe)

                def h_transpose(s, b):
                    ps = fill(pe, s.u, "h_t", s.i(b))
                    pe.wait_ge(xs_loaded[s.p][b], 32 * (s.u + 1))
                    for k in range(KC):
                        last = pe.transpose(ps[:, P * k:P * k + P], xs[:, s.p, b, k, :], ident[:, :])
                    last.then_inc(done["h_t"], 1)

                def qkv(s, b):
                    parts = [(h_hi[:, b % 2, k, :], h_lo[:, b % 2, k, :]) for k in range(KC)]
                    for a in range(3):
                        kind, i = ("qk", 2 * s.i(b) + a) if a < 2 else ("v", s.i(b))
                        ps = fill(pe, s.u, kind, i)
                        if a == 0:
                            pe.wait_ge(h_ready, s.n(b) + 1)
                        cols = slice(INNER * a, INNER * a + INNER)
                        split3(pe, ps[:, :], parts, [(wqkv[0][:, k, cols], wqkv[1][:, k, cols]) for k in range(KC)]).then_inc(done[kind], 1)

                def qk_transpose(s, b):
                    for kind, c in (("q_t", 0), ("k_t", INNER)):
                        ps = fill(pe, s.u, kind, s.i(b))
                        pe.wait_ge(rot_ready, s.n(b) + 1)
                        rows = t1[:, :, :].rearrange("p h d -> p (h d)")
                        for j in range(PAIRS):
                            last = pe.transpose(ps[:, P * j:P * j + P], rows[:, c + P * j:c + P * j + P], ident[:, :])
                        last.then_inc(done[kind], 1)

                def scores(s, r):
                    b, j = divmod(r, PAIRS)
                    ps = fill(pe, s.u, "s", B * PAIRS * s.p + r)
                    pe.wait_ge(qt_ready, 2 * s.n(b) + 2)
                    pe.wait_ge(kt_ready, s.n(b) + 1)
                    for e in range(2):
                        last = pe.matmul(ps[:, 2 * P * e:2 * P * e + 2 * P], qt[:, b % 2, 2 * j + e, :],
                                         kt[:, b, j].rearrange("p w n -> p (w n)"), start=True, stop=True)
                    last.then_inc(done["s"], 1)

                def p_transpose(s, r):
                    ps = fill(pe, s.u, "p_t", B * PAIRS * s.p + r)
                    pe.wait_ge(pn_ready, (2 * s.u + s.p) * B * PAIRS + r + 1)
                    for e in range(2):
                        for w in range(2):
                            c = P * (2 * e + w)
                            last = pe.transpose(ps[:, c:c + P], sm[:, r % 4, e, P * w:P * w + P], ident[:, :])
                    last.then_inc(done["p_t"], 1)

                def values(s, r):
                    b, j = divmod(r, PAIRS)
                    if j == 0:
                        fill(pe, s.u, "o", s.i(b))
                        pe.wait_ge(v_ready, s.n(b) + 1)
                    pe.wait_ge(pt_ready, (2 * s.u + s.p) * B * PAIRS + r + 1)
                    for e in range(2):
                        c = HD * (2 * j + e)
                        for w in range(2):
                            last = pe.matmul(banks[f"O{b % 2}"][HD * e:HD * e + HD, P * j:P * j + P], vt[:, b, w, c:c + HD],
                                             pt[:, r % 2, 2 * e + w, :], start=(w == 0), stop=(w == 1))
                    last.then_inc(pv_done, 1)

                def project(s, b):
                    ps = fill(pe, s.u, "wo", s.i(b))
                    pe.wait_ge(o_ready, s.n(b) + 1)
                    split3(pe, ps[:, 0:D], [(o_hi[:, b % 2, c, :], o_lo[:, b % 2, c, :]) for c in range(PAIRS)],
                           [(wo[0][:, c, :], wo[1][:, c, :]) for c in range(PAIRS)]).then_inc(done["wo"], 1)

                def x_transpose(s, b):
                    ps = fill(pe, s.u, "x_t", s.i(b))
                    pe.wait_ge(xn_ready[s.p], B * s.u + b + 1)
                    for k in range(KC):
                        last = pe.transpose(ps[:, P * k:P * k + P], xn[:, b % 2, P * k:P * k + P], ident[:, :])
                    last.then_inc(done["x_t"], 1)

                def hidden(s, kind, j):
                    ps = fill(pe, s.u, kind, NC * s.p + j)
                    c = CO[j] + (HID if kind == "g" else 0)
                    split3(pe, ps[0:CS[j], :], [(w1[0][:, k, c:c + CS[j]], w1[1][:, k, c:c + CS[j]]) for k in range(KC)],
                           [(f_hi[:, k, :], f_lo[:, k, :]) for k in range(KC)]).then_inc(done[kind], 1)

                def outputs(s, j):
                    if j == 0:
                        fill(pe, s.u, "y", 2 * s.p)
                        fill(pe, s.u, "y", 2 * s.p + 1)
                    pe.wait_ge(u_ready, (2 * s.u + s.p) * NC + j + 1)
                    n = CS[j]
                    for b in range(B):
                        ps = banks[f"O{b // 2}"][:, D * (b % 2):D * (b % 2) + D]
                        cols = slice(P * b, P * b + P)
                        pe.matmul(ps, u_hi[0:n, j % 2, cols], w2[0][0:n, j, :], start=(j == 0 and b % 2 == 0), stop=False, skip_group_check=True)
                        pe.matmul(ps, u_hi[0:n, j % 2, cols], w2[1][0:n, j, :], start=False, stop=False, skip_group_check=True)
                        pe.matmul(ps, u_lo[0:n, j % 2, cols], w2[0][0:n, j, :], start=False, stop=(j == NC - 1), skip_group_check=True).then_inc(w2_done, 1)

                def ahead(s, part):
                    if part == 0:
                        h_transpose(s, 0), h_transpose(s, 1)
                    elif part == 1:
                        qkv(s, 0)
                    elif part == 2:
                        h_transpose(s, 2)
                    elif part == 3:
                        qkv(s, 1)
                    else:
                        qk_transpose(s, 0)

                def step(s, following):
                    for r in range(ROUNDS):
                        b, j = divmod(r, PAIRS)
                        if b < B:
                            scores(s, r)
                        if r in (0, PAIRS):
                            qkv(s, b + 2)
                        if 0 <= r - LAG < B * PAIRS:
                            p_transpose(s, r - LAG)
                        if 0 <= r - LAG - 1 < B * PAIRS:
                            values(s, r - LAG - 1)
                        if b + 1 < B and j == 2:
                            qk_transpose(s, b + 1)
                        if r == 3:
                            h_transpose(s, 3)
                        if (b := at(r, 8)) is not None:
                            project(s, b)
                        if (b := at(r, 12)) is not None:
                            x_transpose(s, b)
                        if following and r in (18, 19, 20, 21):
                            ahead(following, r - 18)
                    pe.wait_ge(f_ready, s.n(B))
                    for j in range(NC + 2):
                        if j < NC:
                            hidden(s, "g", j)
                            hidden(s, "a", j)
                        if following and j == 2:
                            ahead(following, 4)
                        if j >= 2:
                            outputs(s, j - 2)

                slots.phase = "first"
                for part in range(5):
                    ahead(Step(l, 0, 0), part)
                slots.phase = "body"
                with pe.Fori(0, TURNS - 1) as tp:
                    step(Step(l, tp, 0), Step(l, tp, 1))
                    step(Step(l, tp, 1), Step(l, tp + 1, 0))
                slots.phase = "last"
                step(Step(l, TURNS - 1, 0), Step(l, TURNS - 1, 1))
                step(Step(l, TURNS - 1, 1), None)


def constants():
    f32 = np.float32
    half = np.arange(0, HD, 2, dtype=f32)
    pos = np.arange(N, dtype=f32)
    freqs = pos[:, None] * (f32(1.0) / f32(10000.0) ** (half / f32(HD)))
    xbase = (half + f32(0.4 * HD)) / f32(1.4 * HD)
    scale = xbase[None, :] ** ((pos[:, None] - N // 2) / f32(P // 2))
    cos, sin = np.cos(freqs), np.sin(freqs)
    tabs = [np.concatenate(t, axis=-1) for f in (scale, 1.0 / scale)
            for t in ((cos * f, cos * f), (-sin * f, sin * f))]
    rope = np.stack(tabs, axis=1).reshape(NT, P, 4, HD)
    q, k = np.arange(P)[:, None], np.arange(P)[None, :]
    own = np.where(k <= q, 0.0, BIG)
    before = np.where(k >= q, 0.0, BIG)
    mask = np.zeros((TURNS, P, 2, 2 * P))
    mask[:, :, 0] = np.concatenate([own, before], axis=1)
    mask[:, :, 1] = np.concatenate([before, own], axis=1)
    mask[0, :, 0, P:] = BIG
    flags = np.array([[float(l == NL - 1)] for l in range(NL)])
    return {k: v.astype(np.float32) for k, v in
            {"ident": np.eye(P), "rope": rope, "mask": mask, "flags": flags}.items()}


def build(nc, io, out, kind="Internal"):
    def dram(name, shape):
        return nc.dram_tensor(name, shape, F32, kind=kind).ap() if kind != "Internal" else nc.dram_tensor(name, shape, F32).ap()

    scratch = {
        "mod": dram("mod_rows", (B, 6 * D)),
        "gate": dram("gate_rows", (2, B, D)),
        "x": dram("x_layers", (3, B, N + 1, D)),
        "xa": dram("x_attended", (B, N + 1, D)),
        "base": dram("base_rows", (B, N, D)),
    }
    with ExitStack() as ctx:
        def sb(name, shape, dt=F32):
            return ctx.enter_context(nc.sbuf_tensor(name, shape, dt))

        ident = sb("ident", [P, P])
        with ExitStack() as inner:
            def sb1(name, shape, dt=F32):
                return inner.enter_context(nc.sbuf_tensor(name, shape, dt))

            w = {"ident": ident, "hi": sb1("wt_hi", [P, KC, 4 * D], F32R), "lo": sb1("wt_lo", [P, KC, 4 * D], F32R),
                 "gamma": sb1("gamma", [P, 2, HD]), "bo": sb1("bo", [P, D]), "ln": sb1("ln_cols", [P, 2, KC])}
            setup_block(nc, io, scratch, w)
            attention_block(nc, io, scratch, w)
        layers_block(nc, io, scratch, out, ident)


_INS = {"x": "L0_attn_x", "ln_gamma": "L0_attn_ln_gamma", "ln_beta": "L0_attn_ln_beta", "q_gamma": "L0_attn_q_gamma",
        "k_gamma": "L0_attn_k_gamma", "wq": "L0_attn_w_q", "wk": "L0_attn_w_k", "wv": "L0_attn_w_v",
        "wo": "L0_attn_w_o", "bo": "L0_attn_b_o", "wqkv": "L0_ffn_wqkv", "q_scale": "L0_ffn_q_scale",
        "k_scale": "L0_ffn_k_scale", "f_wo": "L0_ffn_wo", "lg": "L0_ffn_ln_g", "lb": "L0_ffn_ln_b",
        "w1": "L0_ffn_w1", "b1": "L0_ffn_b1", "w2": "L0_ffn_w2", "b2": "L0_ffn_b2", "c": "L0_c", "wmod": "L0_wmod"}


def kernel(**inputs):
    import concourse.bacc as bacc
    from concourse.bass_utils import run_bass_kernel_spmd

    nc = bacc.Bacc("TRN2", target_bir_lowering=False, num_devices=1)
    arrays = {f"in_{k}": np.ascontiguousarray(inputs[name]) for k, name in _INS.items()}
    arrays.update({f"in_{k}": v for k, v in constants().items()})
    io = {k[3:]: nc.dram_tensor(k, a.shape, mybir.dt.from_np(a.dtype), kind="ExternalInput").ap() for k, a in arrays.items()}
    out = nc.dram_tensor("out_0", (B, N, D), F32, kind="ExternalOutput").ap()
    build(nc, io, out)
    result = run_bass_kernel_spmd(nc, [arrays], core_ids=[0])
    return result.results[0]["out_0"]
```
